# Optimizing a Trainium2 kernel written in Bass

```python
import numpy as np
import jax
import jax.numpy as jnp

def _softmax(x, axis=-1):
    return jax.nn.softmax(x, axis=axis)

def _gelu(x):
    return jax.nn.gelu(x, approximate=True)

def _silu(x):
    return jax.nn.silu(x)

def _sigmoid(x):
    return jax.nn.sigmoid(x)

def _layernorm(x, axis=-1, eps=1e-05):
    m = jnp.mean(x, axis=axis, keepdims=True)
    v = jnp.var(x, axis=axis, keepdims=True)
    return (x - m) / jnp.sqrt(v + eps)

def _scatter_add(tgt, idx, src, axis=0):
    return tgt.at[idx].add(src)

def _segment_sum(src, seg, n):
    return jax.ops.segment_sum(src, seg, n)
kernel_name = 'mk_decoder_postln_d1_seqx_r8_b4d205'

def setup_inputs(seed: int=0):
    np.random.seed(seed)
    _w = jnp.asarray

    def _rec_inputs():
        import jax
        import jax.numpy as jnp
        _rk = jax.random.key(seed)
        x = -0.0002928 + 1 * jax.random.normal(jax.random.fold_in(_rk, 1), (32, 64, 128), jnp.float32)
        _lenS = 64 - jax.random.randint(jax.random.fold_in(_rk, 7), (32,), 0, max(1, 64 // 4) + 1, jnp.int32)
        _lenS2 = 64 - jax.random.randint(jax.random.fold_in(_rk, 8), (32,), 0, max(1, 64 // 4) + 1, jnp.int32)
        _ctx_1024P = jax.random.normal(jax.random.fold_in(_rk, 11), (32, 16, 128), jnp.float32)
        _ctx_1024c = jax.random.dirichlet(jax.random.fold_in(_rk, 511), 0.3 * jnp.ones((16,), jnp.float32), (32, 64))
        _ctx_1024t = jnp.einsum('bsk,bkd->bsd', _ctx_1024c, _ctx_1024P)
        _ctx_1024t = _ctx_1024t * jax.lax.rsqrt(jnp.mean(jnp.square(_ctx_1024t)) + 1e-12) * 0.953939
        ctx_1024 = -1.39393e-06 + 0.999914 * (_ctx_1024t + 0.3 * jax.random.normal(jax.random.fold_in(_rk, 611), (32, 64, 128), jnp.float32))
        return (x, ctx_1024)
    x, ctx_1024 = _rec_inputs()

    def _L0_attn_setup():
        import jax, jax.numpy as jnp
        import numpy as np
        EPS = 1e-06
        N_HEADS = 16

        def _stable_softmax(x):
            x_max = jax.lax.stop_gradient(jnp.max(x, axis=-1, keepdims=True))
            exp_x = jnp.exp(jnp.clip(x - x_max, -50.0, 50.0))
            return exp_x / (jnp.sum(exp_x, axis=-1, keepdims=True) + EPS)
        key = jax.random.key(seed)
        k1, k2, k3 = jax.random.split(key, 3)
        B, S, D = (2, 256, 128)
        x = jax.random.normal(k1, (B, S, D), dtype=jnp.float32)
        Wqkv = jax.random.normal(k2, (3 * D, D), dtype=jnp.float32) * 0.02
        Wout = jax.random.normal(k3, (D, D), dtype=jnp.float32) * (0.02 / np.sqrt(2))
        return {'x': x, 'Wqkv': Wqkv, 'Wout': Wout}
    _L0_attn_all = _L0_attn_setup()
    _L0_attn_in = {k: v for k, v in _L0_attn_all.items() if k in ('Wqkv', 'Wout')}
    del _L0_attn_all

    def _L0_xattn_setup():
        import jax, jax.numpy as jnp
        import numpy as np
        DIM = 128
        N_HEADS = 16
        HEAD_DIM = DIM // N_HEADS
        B, N, M = (2, 256, 256)
        key = jax.random.key(seed)
        ks = jax.random.split(key, 10)
        s = 1.0 / np.sqrt(DIM)
        return {'x1': jax.random.normal(ks[0], (B, N, DIM), dtype=jnp.float32), 'x2': jax.random.normal(ks[1], (B, M, DIM), dtype=jnp.float32), 'Wq': jax.random.normal(ks[2], (DIM, DIM), dtype=jnp.float32) * s, 'bq': jnp.zeros((DIM,), dtype=jnp.float32), 'Wk': jax.random.normal(ks[3], (DIM, DIM), dtype=jnp.float32) * s, 'bk': jnp.zeros((DIM,), dtype=jnp.float32), 'Wv': jax.random.normal(ks[4], (DIM, DIM), dtype=jnp.float32) * s, 'bv': jnp.zeros((DIM,), dtype=jnp.float32), 'Wo': jax.random.normal(ks[5], (DIM, DIM), dtype=jnp.float32) * s, 'bo': jnp.zeros((DIM,), dtype=jnp.float32)}
    _L0_xattn_all = _L0_xattn_setup()
    _L0_xattn_in = {k: v for k, v in _L0_xattn_all.items() if k in ('Wq', 'bq', 'Wk', 'bk', 'Wv', 'bv', 'Wo', 'bo')}
    del _L0_xattn_all

    def _L0_ffn_setup():
        import jax, jax.numpy as jnp
        import numpy as np
        K = 2
        CAP_FACTOR = 1.25
        key = jax.random.key(seed)
        ks = jax.random.split(key, 6)
        B, T, C, H, E = (8, 256, 128, 512, 8)
        return {'x': jax.random.normal(ks[0], (B, T, C), dtype=jnp.float32), 'Wr': jax.random.normal(ks[1], (C, E), dtype=jnp.float32) * 0.02, 'W1': jax.random.normal(ks[2], (E, C, H), dtype=jnp.float32) * 0.02, 'b1': jax.random.normal(ks[3], (E, H), dtype=jnp.float32) * 0.02, 'W2': jax.random.normal(ks[4], (E, H, C), dtype=jnp.float32) * 0.02, 'b2': jax.random.normal(ks[5], (E, C), dtype=jnp.float32) * 0.02}
    _L0_ffn_all = _L0_ffn_setup()
    _L0_ffn_in = {k: v for k, v in _L0_ffn_all.items() if k in ('Wr', 'W1', 'b1', 'W2', 'b2')}
    del _L0_ffn_all
    return {'x': x, 'ctx_1024': ctx_1024, 'L0_attn_Wqkv': _L0_attn_in['Wqkv'], 'L0_attn_Wout': _L0_attn_in['Wout'], 'L0_xattn_Wq': _L0_xattn_in['Wq'], 'L0_xattn_bq': _L0_xattn_in['bq'], 'L0_xattn_Wk': _L0_xattn_in['Wk'], 'L0_xattn_bk': _L0_xattn_in['bk'], 'L0_xattn_Wv': _L0_xattn_in['Wv'], 'L0_xattn_bv': _L0_xattn_in['bv'], 'L0_xattn_Wo': _L0_xattn_in['Wo'], 'L0_xattn_bo': _L0_xattn_in['bo'], 'L0_ffn_Wr': _L0_ffn_in['Wr'], 'L0_ffn_W1': _L0_ffn_in['W1'], 'L0_ffn_b1': _L0_ffn_in['b1'], 'L0_ffn_W2': _L0_ffn_in['W2'], 'L0_ffn_b2': _L0_ffn_in['b2']}

def reference(x, ctx_1024, L0_attn_Wqkv, L0_attn_Wout, L0_xattn_Wq, L0_xattn_bq, L0_xattn_Wk, L0_xattn_bk, L0_xattn_Wv, L0_xattn_bv, L0_xattn_Wo, L0_xattn_bo, L0_ffn_Wr, L0_ffn_W1, L0_ffn_b1, L0_ffn_W2, L0_ffn_b2):
    import jax
    import jax.numpy as jnp

    def _L0_attn_ref(x, Wqkv, Wout):
        import jax, jax.numpy as jnp
        import numpy as np
        EPS = 1e-06
        N_HEADS = 16

        def _stable_softmax(x):
            x_max = jax.lax.stop_gradient(jnp.max(x, axis=-1, keepdims=True))
            exp_x = jnp.exp(jnp.clip(x - x_max, -50.0, 50.0))
            return exp_x / (jnp.sum(exp_x, axis=-1, keepdims=True) + EPS)
        B, S, D = x.shape
        H = N_HEADS
        Dh = D // H
        scale = 1.0 / np.sqrt(Dh)
        qkv = (x @ Wqkv.T).reshape(B, S, 3, H, Dh)
        qkv = jnp.transpose(qkv, (2, 0, 3, 1, 4))
        q, k, v = (qkv[0], qkv[1], qkv[2])
        scores = jnp.einsum('bhqd,bhkd->bhqk', q, k) * scale
        attn = _stable_softmax(scores)
        out = jnp.einsum('bhqk,bhkd->bhqd', attn, v)
        out = jnp.transpose(out, (0, 2, 1, 3)).reshape(B, S, D)
        return out @ Wout.T

    def _L0_xattn_ref(x1, x2, Wq, bq, Wk, bk, Wv, bv, Wo, bo):
        import jax, jax.numpy as jnp
        import numpy as np
        DIM = 128
        N_HEADS = 16
        HEAD_DIM = DIM // N_HEADS
        B, N, M = (2, 256, 256)
        b, n, _ = x1.shape
        m = x2.shape[1]
        q = x1 @ Wq.T + bq
        k = x2 @ Wk.T + bk
        v = x2 @ Wv.T + bv
        q = q.reshape(b, n, N_HEADS, HEAD_DIM).transpose(0, 2, 1, 3)
        k = k.reshape(b, m, N_HEADS, HEAD_DIM).transpose(0, 2, 1, 3)
        v = v.reshape(b, m, N_HEADS, HEAD_DIM).transpose(0, 2, 1, 3)
        scale = 1.0 / jnp.sqrt(jnp.asarray(HEAD_DIM, dtype=q.dtype))
        scores = jnp.einsum('bhnd,bhmd->bhnm', q, k) * scale
        attn = jax.nn.softmax(scores, axis=-1)
        o = jnp.einsum('bhnm,bhmd->bhnd', attn, v)
        o = o.transpose(0, 2, 1, 3).reshape(b, n, DIM)
        return o @ Wo.T + bo

    def _L0_ffn_ref(x, Wr, W1, b1, W2, b2):
        import jax, jax.numpy as jnp
        import numpy as np
        K = 2
        CAP_FACTOR = 1.25
        B, T, C = x.shape
        E = Wr.shape[1]
        capacity = int(T / E * CAP_FACTOR)
        probs = jax.nn.softmax(x @ Wr, axis=-1)
        topk_probs, topk_experts = jax.lax.top_k(probs, K)
        S = T * K
        e_flat = topk_experts.reshape(B, S)
        p_flat = topk_probs.reshape(B, S)
        x_rep = jnp.repeat(x, K, axis=1)
        onehot = jax.nn.one_hot(e_flat, E, dtype=jnp.int32)
        pos_all = jnp.cumsum(onehot, axis=1) - onehot
        pos = jnp.take_along_axis(pos_all, e_flat[..., None], axis=-1)[..., 0]
        keep = pos < capacity
        pos_c = jnp.minimum(pos, capacity - 1)
        b_idx = jnp.broadcast_to(jnp.arange(B)[:, None], (B, S))
        buf = jnp.zeros((E, B, capacity, C), dtype=x.dtype)
        buf = buf.at[e_flat, b_idx, pos_c].add(x_rep * keep[..., None].astype(x.dtype))
        h = jax.nn.relu(jnp.einsum('ebnc,ech->ebnh', buf, W1) + b1[:, None, None, :])
        y = jnp.einsum('ebnh,ehc->ebnc', h, W2) + b2[:, None, None, :]
        y_tok = y[e_flat, b_idx, pos_c]
        y_tok = y_tok * keep[..., None].astype(x.dtype) * p_flat[..., None]
        out = y_tok.reshape(B, T, K, C).sum(axis=2)
        return out
    x = _layernorm(x + _L0_attn_ref(x, L0_attn_Wqkv, L0_attn_Wout), axis=-1)
    x = _layernorm(x + _L0_xattn_ref(x, ctx_1024, L0_xattn_Wq, L0_xattn_bq, L0_xattn_Wk, L0_xattn_bk, L0_xattn_Wv, L0_xattn_bv, L0_xattn_Wo, L0_xattn_bo), axis=-1)
    x = _layernorm(x + _L0_ffn_ref(x, L0_ffn_Wr, L0_ffn_W1, L0_ffn_b1, L0_ffn_W2, L0_ffn_b2), axis=-1)
    return x

_drawn_inputs = setup_inputs


def setup_inputs(seed=0):
    import zlib

    import numpy as np

    out = dict(_drawn_inputs(seed))
    spreads = {'L0_xattn_bq': (0.0, 0.335),
     'L0_xattn_bk': (0.0, 0.8),
     'L0_xattn_bv': (0.0, 0.1),
     'L0_xattn_bo': (0.0, 0.1)}
    factors = {'L0_attn_Wqkv': 8.0,
     'L0_attn_Wout': 8.0,
     'L0_ffn_Wr': 5.007,
     'L0_ffn_W1': 5.738,
     'L0_ffn_b1': 8.0,
     'L0_ffn_W2': 4.682,
     'L0_ffn_b2': 8.0}
    for name, (base, spread) in spreads.items():
        noise = np.random.default_rng([zlib.crc32(name.encode()), seed]).standard_normal(out[name].shape)
        drawn = base * np.exp(spread * noise) if base else spread * noise
        out[name] = jnp.asarray(drawn.astype(out[name].dtype))
    for name, factor in factors.items():
        out[name] = (out[name] * factor).astype(out[name].dtype)
    return out
```

```python
from contextlib import ExitStack

import concourse.bass as bass
from concourse import mybir
import numpy as np

F32 = mybir.dt.float32
ALU = mybir.AluOpType
ACT = mybir.ActivationFunctionType
AX = mybir.AxisListType

P = 128
BATCH, SEQ, D = 32, 64, 128
PAIRS = BATCH // 2
HEADS, DH = 16, 8
SCALE = 1.0 / float(np.sqrt(DH))
SOFTMAX_EPS = 1e-6
CLIP_FLOOR = float(np.exp(-50.0))
LN_EPS = 1e-5
E = 8
FF = 512
FJ = FF // P
TOPK = 2
CAP = int(SEQ / E * 1.25)
PSLOT = 2 * CAP
ESLOT = PAIRS * PSLOT
DSLOT = E * PSLOT
BSLOT = E * CAP
A, B = 0, 1


def need(eng, sem, count):
    if isinstance(count, int) and count <= 0:
        return
    eng.wait_ge(sem, count)


def capped(n):
    return min(n, PAIRS) if isinstance(n, int) else n


def peeled(eng, count, body, first=1):
    for m in range(first):
        body(m)
    with eng.Fori(first, count) as m:
        body(m)


def pipeline(eng, iteration):
    def run(i):
        live = lambda u: not isinstance(u, int) or 0 <= u < PAIRS
        units = (i, i - 2, i - 1, i - 3)
        iteration(*[u if live(u) else None for u in units])
    for i in range(4):
        run(i)
    with eng.Fori(4, PAIRS) as i:
        run(i)
    for i in range(PAIRS, PAIRS + 3):
        run(i)


def decoder_kernel(nc, t_in, out):
    with ExitStack() as ctx:
        def sb(name, shape):
            return ctx.enter_context(nc.sbuf_tensor(name, shape, F32))

        def sem(name):
            return ctx.enter_context(nc.semaphore(name))

        def sem2(name):
            return [sem(name + "_self"), sem(name + "_cross")]

        xT = sb("xT", [P, PAIRS * P])
        cT = sb("cT", [P, PAIRS * P])
        xnat = sb("xnat", [P, PAIRS, D])
        x1b_all = sb("x1b_all", [P, PAIRS, D])
        x2_all = sb("x2_all", [P, PAIRS, D])
        logits = sb("logits", [P, PAIRS, E])
        ident = sb("ident", [P, P])
        hmask = sb("hmask", [P, 4, SEQ])
        before = sb("before", [P, P])
        rank = sb("rank", [P, E])
        slotno = sb("slotno", [P, PSLOT])
        wq = [sb("wq_self", [P, D]), sb("wq_cross", [P, D])]
        wk = [sb("wk_self", [P, D]), sb("wk_cross", [P, D])]
        wv = [sb("wv_self", [P, D]), sb("wv_cross", [P, D])]
        wo = [sb("wo_self", [P, 2, D]), sb("wo_cross", [P, 2, D])]
        wo_full = sb("wo_full", [P, D])
        bias = sb("bias", [P, 4])
        bo_row = sb("bo_row", [1, D])
        ones_row = sb("ones_row", [1, P])
        bv_cols = sb("bv_cols", [P, P])
        bo_all = sb("bo_all", [P, D])
        wr = sb("wr", [P, E])
        b1 = sb("b1", [P, E, FJ])
        b2 = sb("b2", [P, E])
        mhalf = sb("mhalf", [P, 1])
        xs = [sb(f"xs{n}", [P, 2, 2, SEQ]) for n in (A, B)]
        x1T = sb("x1T", [P, 2, SEQ])
        QZ = [sb(f"QZ{n}", [P, 2, 4, SEQ]) for n in (A, B)]
        KM = [sb(f"KM{n}", [P, 2, 4, SEQ]) for n in (A, B)]
        VB = [sb(f"VB{n}", [P, 2, 2, 2, 2, 18]) for n in (A, B)]
        MX = [sb(f"MX{n}", [P, 2, 8]) for n in (A, B)]
        PZ = [sb(f"PZ{n}", [P, 2, 8, SEQ]) for n in (A, B)]
        PT = [sb(f"PT{n}", [P, 2, 4, P]) for n in (A, B)]
        DEN = [sb(f"DEN{n}", [P, 8, 2]) for n in (A, B)]
        REC = [sb(f"REC{n}", [P, 8, 2]) for n in (A, B)]
        ON = [sb(f"ON{n}", [P, 8, 2, 8]) for n in (A, B)]
        OT = [sb(f"OT{n}", [P, 2, SEQ]) for n in (A, B)]
        R = [sb(f"R{n}", [P, D]) for n in (A, B)]
        ST = [sb(f"ST{n}", [P, 6]) for n in (A, B)]
        MV = [sb(f"MV{n}", [P, 2]) for n in (A, B)]
        VE = [sb(f"VE{n}", [P, 1]) for n in (A, B)]
        RS = [sb(f"RS{n}", [P, 1]) for n in (A, B)]
        XN = [sb(f"XN{n}", [P, D]) for n in (A, B)]
        x2T = sb("x2T", [P, P])
        rmax = sb("rmax", [P, PAIRS])
        rz = sb("rz", [P, PAIRS, E])
        prob = sb("prob", [P, PAIRS, E])
        pick = [sb(f"pick{k}", [P, PAIRS, E]) for k in range(TOPK)]
        cand = sb("cand", [P, PAIRS, E])
        chosen = sb("chosen", [P, PAIRS, E])
        gate = sb("gate", [P, PAIRS, E])
        place = sb("place", [P, PAIRS, E])
        disp = sb("disp", [P, PAIRS, E, PSLOT])
        gdisp = sb("gdisp", [P, PAIRS, E, PSLOT])
        x2s = [sb(f"x2s{n}", [P, D]) for n in range(2)]
        buf = sb("buf", [P, E, ESLOT])
        yexp = sb("yexp", [P, E, ESLOT])
        w1 = [sb(f"w1_{n}", [P, FF]) for n in range(2)]
        w2 = [sb(f"w2_{n}", [P, FJ, D]) for n in range(2)]
        HT = [sb(f"HT{n}", [P, FJ, ESLOT]) for n in range(2)]
        yg_in = [sb(f"yg_in{n}", [P, 4, BSLOT]) for n in range(2)]
        yg = [sb(f"yg{n}", [P, 4, P]) for n in range(2)]
        res = [sb(f"res{n}", [P, D]) for n in range(2)]

        bank = [ctx.enter_context(nc.psum_tensor(f"bank{n}", [P, 512], F32)) for n in range(8)]
        S_bank = [bank[0], bank[1]]
        PT_bank = [bank[2], bank[3]]
        QV_bank = bank[4]
        K_bank = bank[5]
        O_bank = bank[6]
        Y_bank = bank[7]

        first_in, rest_in, out_done = sem("first_in"), sem("rest_in"), sem("out_done")
        w_in = [sem("w_in0"), sem("w_in1")]
        zero_ready, ones_ready, bv_ready = sem("zero_ready"), sem("ones_ready"), sem("bv_ready")
        bo_sum, bo_ready = sem("bo_sum"), sem("bo_ready")
        xs_ready = sem2("xs_ready")
        qv_done, k_done = sem2("qv_done"), sem2("k_done")
        qz_ready, vb_ready, km_ready = sem2("qz_ready"), sem2("vb_ready"), sem2("km_ready")
        s_done, mx_ready, z_ready, p_ready = sem2("s_done"), sem2("mx_ready"), sem2("z_ready"), sem2("p_ready")
        t_done, pt_ready, pv_done = sem2("t_done"), sem2("pt_ready"), sem2("pv_done")
        den_ready, rec_ready, on_ready = sem2("den_ready"), sem2("rec_ready"), sem2("on_ready")
        ot_done, ot_ready, y_done = sem2("ot_done"), sem2("ot_ready"), sem2("y_done")
        r_ready, st_ready, mv_ready, ve_ready = sem2("r_ready"), sem2("st_ready"), sem2("mv_ready"), sem2("ve_ready")
        rs_ready, xn_ready, xt_done, xt_ready = sem2("rs_ready"), sem2("xn_ready"), sem2("xt_done"), sem2("xt_ready")
        x1b_ready, x2_kept, lg_done, lg_ready = sem("x1b_ready"), sem("x2_kept"), sem("lg_done"), sem("lg_ready")

        ye_done = [sem("ye_done0"), sem("ye_done1")]
        h_done, h_ready_act, h_ready_dve = sem("h_done"), sem("h_ready_act"), sem("h_ready_dve")
        y_ready = [sem("yexp_ready0"), sem("yexp_ready1")]
        x2s_ready = [sem("x2s_ready0"), sem("x2s_ready1")]
        d_done = [sem("d_done0"), sem("d_done1")]
        buf_ready = [sem("buf_ready0"), sem("buf_ready1")]
        ygin_ready = [sem("ygin_ready0"), sem("ygin_ready1")]
        ygt_done = [sem("ygt_done0"), sem("ygt_done1")]
        yg_ready = [sem("yg_ready0"), sem("yg_ready1")]
        c_done = [sem("c_done0"), sem("c_done1")]
        fr_ready, fst, fmv = [sem("fr0"), sem("fr1")], [sem("fst0"), sem("fst1")], [sem("fmv0"), sem("fmv1")]
        fve, frs, res_ready = [sem("fve0"), sem("fve1")], [sem("frs0"), sem("frs1")], [sem("res0"), sem("res1")]
        router, rz_ready, rexp_ready = sem("router"), sem("rz_ready"), sem("rexp_ready")
        chosen_ready, pos_done, disp_ready, gdisp_ready = sem("chosen_ready"), sem("pos_done"), sem("disp_ready"), sem("gdisp_ready")

        def headed(ap, n):
            return ap.unsqueeze(1).broadcast_to([ap.shape[0], n, *ap.shape[1:]])

        xt_view = [t[:, :].rearrange("p (u b k) -> p u b k", b=2, k=SEQ) for t in (xT, cT)]
        O_view = O_bank[:, 0:288].rearrange("p (n g h d) -> p n g h d", n=8, g=2, h=2)

        block = ctx.enter_context(nc.Block())

        @block.sync
        def _(sp):
            def load(dst, name, s, view=None):
                src = t_in[name] if view is None else view
                sp.dma_start(dst, src).then_inc(s, 16)
                return 1
            half = PAIRS * P // 8
            n = load(xT[:, 0:half], "xT", first_in, t_in["xT"][:, 0:half])
            n += load(wq[A][:], "wq_self", first_in) + load(wk[A][:], "wk_self", first_in)
            n += load(wv[A][:], "wv_self", first_in) + load(hmask[:], "hmask", first_in)
            n += load(ident[:], "ident", first_in)
            assert n == FIRST
            n = load(wo[A][:], "wo_self", rest_in) + load(xnat[:], "xnat", rest_in)
            n += load(xT[:, half:], "xT", rest_in, t_in["xT"][:, half:])
            n += load(cT[:], "cT", rest_in)
            for dst, name in ((wq[B], "wq_cross"), (wk[B], "wk_cross"), (wv[B], "wv_cross"), (wo[B], "wo_cross"),
                              (wo_full, "wo_full"), (bias, "bias"), (bo_row, "bo_row"), (wr, "wr"), (b1, "b1"),
                              (b2, "b2"), (before, "before"), (rank, "rank"), (slotno, "slotno")):
                n += load(dst[:], name, rest_in)
            assert n == REST
            def weights(e, k):
                sp.dma_start(w1[k][:], t_in["w1"][bass.ds(e, 1)].rearrange("o c f -> c (o f)")).then_inc(w_in[k], 16)
                sp.dma_start(w2[k][:], t_in["w2"][bass.ds(e, 1)].rearrange("o (j p) c -> p (o j) c", p=P)).then_inc(w_in[k], 16)
            weights(0, 0)
            weights(1, 1)
            with sp.Fori(1, E // 2) as m:
                for k in range(2):
                    sp.wait_ge(ye_done[k], m)
                    weights(2 * m + k, k)
            with sp.Fori(0, PAIRS // 2) as m:
                for k in range(2):
                    sp.wait_ge(res_ready[k], m + 1)
                    sp.dma_start(out[bass.ds(2 * m + k, 1)].rearrange("o t c -> t (o c)"), res[k][:]).then_inc(out_done, 16)
            sp.wait_ge(out_done, 16 * PAIRS)

        @block.gpsimd
        def _(pool):
            for n in (A, B):
                nc.gpsimd.memset(QZ[n][:], 0.0)
                nc.gpsimd.memset(VB[n][:], 0.0)
            nc.gpsimd.memset(mhalf[:], -0.5)
            nc.gpsimd.memset(ones_row[:], 1.0).then_inc(zero_ready, 1)
            pool.wait_ge(zero_ready, 1)
            for hl in range(2):
                for n in (A, B):
                    ones = VB[n][:].rearrange("p b g l h (e j) -> p (b g l h) e j", e=2)
                    last = nc.gpsimd.memset(ones[64 * hl:64 * hl + 64, :, hl, DH:DH + 1], 1.0)
                last.then_inc(ones_ready, 1)
                pool.wait_ge(ones_ready, hl + 1)
            pool.wait_ge(rest_in, 16 * REST)
            nc.gpsimd.tensor_copy(bv_cols[:], bias[:, 2:3].broadcast_to([P, P])).then_inc(bv_ready, 1)

            def stage(n, u):
                need(pool, k_done[n], u)
                src = xt_view[n][:, bass.ds(u, 1)].rearrange("p o b k -> p (o b) k")
                nc.gpsimd.tensor_copy(xs[n][:], src.unsqueeze(2).broadcast_to([P, 2, 2, SEQ])).then_inc(xs_ready[n], 1)

            def power(n, u):
                need(pool, ve_ready[n], u + 1)
                nc.gpsimd.tensor_tensor(RS[n][:], VE[n][:], mhalf[:], ALU.pow).then_inc(rs_ready[n], 1)

            def iteration(ha, hb, ta, tb):
                if ha is not None:
                    stage(A, ha)
                if hb is not None:
                    stage(B, hb)
                if ta is not None:
                    power(A, ta)
                    need(pool, bo_ready, 1) if isinstance(ta, int) else None
                    need(pool, xn_ready[A], ta + 1)
                    nc.gpsimd.tensor_tensor(x1b_all[:, bass.ds(ta, 1)].rearrange("p o c -> p (o c)"), XN[A][:],
                                            bo_all[:], ALU.add).then_inc(x1b_ready, 1)
                if tb is not None:
                    power(B, tb)
                    need(pool, xn_ready[B], tb + 1)
                    nc.gpsimd.tensor_copy(x2_all[:, bass.ds(tb, 1)].rearrange("p o c -> p (o c)"), XN[B][:])\
                        .then_inc(x2_kept, 1)

            pipeline(pool, iteration)

            pool.wait_ge(x2_kept, PAIRS)
            def copy_x2(p, k):
                nc.gpsimd.tensor_copy(x2s[k][:], x2_all[:, bass.ds(p, 1)].rearrange("p o c -> p (o c)"))\
                    .then_inc(x2s_ready[k], 1)
            for k in range(2):
                copy_x2(k, k)
            with pool.Fori(1, PAIRS // 2) as m:
                for k in range(2):
                    pool.wait_ge(d_done[k], m)
                    copy_x2(2 * m + k, k)
            pool.wait_ge(gdisp_ready, 1)
            for k in range(2):
                pool.wait_ge(y_ready[k], E // 2)
            yv = yexp[:].rearrange("p e (u b s) -> p u b e s", b=2, s=CAP)
            gv = gdisp[:].rearrange("p u e (b s) -> p u b e s", b=2)
            def copy_yg(p, k):
                d = yg_in[k][:].rearrange("p n (e s) -> p n e s", s=CAP)
                for b in range(2):
                    nc.gpsimd.tensor_copy(d[:, b], yv[:, bass.ds(p, 1), b].rearrange("p o e s -> p (o e) s"))
                    last = nc.gpsimd.tensor_copy(d[:, 2 + b], gv[:, bass.ds(p, 1), b].rearrange("p o e s -> p (o e) s"))
                last.then_inc(ygin_ready[k], 1)
            def final_power(k, m):
                pool.wait_ge(fve[k], m + 1)
                nc.gpsimd.tensor_tensor(RS[k][:], VE[k][:], mhalf[:], ALU.pow).then_inc(frs[k], 1)
            for k in range(2):
                copy_yg(k, k)
            with pool.Fori(1, PAIRS // 2) as m:
                for k in range(2):
                    pool.wait_ge(ygt_done[k], m)
                    copy_yg(2 * m + k, k)
                    final_power(k, m - 1)
            for k in range(2):
                final_power(k, PAIRS // 2 - 1)

        @block.scalar
        def _(act):
            def spread_queries(n, u):
                need(act, qv_done[n], u + 1)
                need(act, s_done[n], 2 * u)
                for g in range(4):
                    r = slice(32 * g, 32 * g + 32)
                    src = QV_bank[r, 0:P].rearrange("p (b q) -> p b q", b=2)
                    if n == A:
                        last = nc.scalar.activation(QZ[n][r, :, g], src, ACT.Copy)
                    else:
                        last = nc.scalar.activation(QZ[n][r, :, g], src, ACT.Identity, bias=bias[r, 0:1])
                last.then_inc(qz_ready[n], 1)

            def spread_values(n, u):
                need(act, pv_done[n], 2 * u)
                src = QV_bank[:, P:3 * P].rearrange("p (m h d) -> p m h d", h=2, d=DH)
                dst = VB[n][:].rearrange("p b g l h (e j) -> p (b g l h) e j", e=2)
                for hl in range(2):
                    r = slice(64 * hl, 64 * hl + 64)
                    last = nc.scalar.activation(dst[r, :, hl, 0:DH], src[r, :, hl], ACT.Copy)
                last.then_inc(vb_ready[n], 1)

            def exponentials(n, u, b):
                need(act, z_ready[n], 2 * u + b + 1)
                nc.scalar.activation(PZ[n][:, b], PZ[n][:, b], ACT.Exp, scale=SCALE).then_inc(p_ready[n], 1)

            def turned_probs(n, u, b):
                need(act, t_done[n], 2 * u + b + 1)
                need(act, pv_done[n], 2 * u + b - 1)
                nc.scalar.activation(PT[n][:, b].rearrange("p m q -> p (m q)"), PT_bank[n][:], ACT.Copy)\
                    .then_inc(pt_ready[n], 1)

            def turned_heads(n, u):
                need(act, ot_done[n], u + 1)
                need(act, y_done[n], u)
                nc.scalar.activation(OT[n][:].rearrange("p g q -> p (g q)"), K_bank[:, P:2 * P], ACT.Copy)\
                    .then_inc(ot_ready[n], 1)

            def turned_x(n, u):
                need(act, xt_done[n], u + 1)
                if n == A:
                    need(act, qv_done[B], u)
                    nc.scalar.activation(x1T[:].rearrange("p b q -> p (b q)"), Y_bank[:, P:2 * P], ACT.Copy)\
                        .then_inc(xt_ready[n], 1)
                else:
                    need(act, lg_done, u)
                    nc.scalar.activation(x2T[:], Y_bank[:, P:2 * P], ACT.Copy).then_inc(xt_ready[n], 1)

            def keep_logits(u):
                need(act, lg_done, u + 1)
                nc.scalar.activation(logits[:, bass.ds(u, 1)].rearrange("p o e -> p (o e)"), Y_bank[:, 2 * P:2 * P + E],
                                     ACT.Copy).then_inc(lg_ready, 1)

            act.wait_ge(first_in, 16 * FIRST)
            act.wait_ge(zero_ready, 1)
            act.wait_ge(ones_ready, 2)

            def iteration(ha, hb, ta, tb):
                if ha is not None:
                    spread_queries(A, ha)
                    spread_values(A, ha)
                if hb is not None:
                    if isinstance(hb, int) and hb == 0:
                        act.wait_ge(rest_in, 16 * REST)
                    spread_queries(B, hb)
                    spread_values(B, hb)
                if ta is not None:
                    turned_heads(A, ta)
                if tb is not None:
                    turned_heads(B, tb)
                for b in range(2):
                    if ha is not None:
                        exponentials(A, ha, b)
                    if hb is not None:
                        exponentials(B, hb, b)
                        turned_probs(B, hb, b)
                if ta is not None:
                    turned_x(A, ta)
                if tb is not None:
                    turned_x(B, tb)
                    keep_logits(tb)

            pipeline(act, iteration)

            act.wait_ge(rz_ready, 1)
            nc.scalar.activation(prob[:], rz[:], ACT.Exp).then_inc(rexp_ready, 1)

            bufv = buf[:].rearrange("p e (u s) -> p u e s", s=PSLOT)
            with act.Fori(0, PAIRS // 2) as m:
                act.wait_ge(d_done[0], m + 1)
                nc.scalar.activation(bufv[:, bass.ds(2 * m, 1)].rearrange("p o e s -> p (o e) s"),
                                     bank[0][:, 0:DSLOT].rearrange("p (e s) -> p e s", s=PSLOT), ACT.Copy).then_inc(buf_ready[0], 1)

            def hidden(e, k, j, m):
                act.wait_ge(h_done, FJ * e + j + 1)
                if not isinstance(m, int) or m > 0:
                    act.wait_ge(ye_done[k], m)
                nc.scalar.activation(HT[k][:, j], bank[j][:, 0:ESLOT], ACT.Relu,
                                     bias=b1[:, bass.ds(e, 1), j]).then_inc(h_ready_act, 1)
            def experts(m):
                for k in range(2):
                    e = 2 * m + k
                    for j in (0, 2):
                        hidden(e, k, j, m)
                    if k == 0:
                        continue
                    act.wait_ge(ye_done[0], m + 1)
                    nc.scalar.activation(yexp[:, bass.ds(2 * m, 1)].rearrange("p o s -> p (o s)"), bank[4][:, 0:ESLOT],
                                         ACT.Identity, bias=b2[:, bass.ds(2 * m, 1)]).then_inc(y_ready[0], 1)
            experts(0)
            with act.Fori(1, E // 2) as m:
                experts(m)

            def keep_turned(m):
                for k in range(2):
                    act.wait_ge(ygt_done[k], m + 1)
                    need(act, c_done[k], m)
                    nc.scalar.activation(yg[k][0:BSLOT].rearrange("p n c -> p (n c)"), bank[k][0:BSLOT, :], ACT.Copy)\
                        .then_inc(yg_ready[k], 1)
            peeled(act, PAIRS // 2, keep_turned)

        @block.tensor
        def _(pe):
            mm = nc.tensor.matmul

            def project(n, u):
                need(pe, xs_ready[n], u + 1)
                if n == A:
                    need(pe, vb_ready[A], u)
                    need(pe, vb_ready[B], u - 2)
                    q_src = xs[A][:, :, 0]
                else:
                    need(pe, vb_ready[A], capped(u + 3))
                    need(pe, vb_ready[B], u)
                    need(pe, xt_ready[A], u + 1)
                    q_src = x1T[:]
                mm(QV_bank[:, 0:P], wq[n][:], q_src, start=True, stop=True)
                for b in range(2):
                    last = mm(QV_bank[:, P * (b + 1):P * (b + 2)], xs[n][:, b], wv[n][:], start=True, stop=True)
                last.then_inc(qv_done[n], 1)
                if n == A:
                    need(pe, km_ready[A], u)
                    need(pe, km_ready[B], u - 2)
                    need(pe, ot_ready[A], u - 1)
                    need(pe, ot_ready[B], u - 3)
                else:
                    need(pe, km_ready[A], capped(u + 3))
                    need(pe, km_ready[B], u)
                    need(pe, ot_ready[A], u + 1)
                    need(pe, ot_ready[B], u - 1)
                mm(K_bank[:, 0:P], wk[n][:], xs[n][:, :, 0], start=True, stop=True).then_inc(k_done[n], 1)

            def scores(n, u, b):
                need(pe, qz_ready[n], u + 1)
                need(pe, km_ready[n], u + 1)
                need(pe, z_ready[n], 2 * u + b)
                for gp in range(2):
                    last = mm(S_bank[n][:, 256 * gp:256 * gp + 256], QZ[n][:, b, 2 * gp:2 * gp + 2], KM[n][:, b],
                              start=True, stop=True)
                last.then_inc(s_done[n], 1)

            def turn_probs(n, u, b):
                need(pe, p_ready[n], 2 * u + b + 1)
                need(pe, pt_ready[n], 2 * u + b)
                for m in range(4):
                    last = nc.tensor.transpose(PT_bank[n][:, P * m:P * m + P], PZ[n][:, b, 2 * m:2 * m + 2].rearrange("p h k -> p (h k)"), ident[:])
                last.then_inc(t_done[n], 1)

            def weigh_values(n, u, b):
                need(pe, pt_ready[n], 2 * u + b + 1)
                need(pe, vb_ready[n], u + 1)
                if n == A:
                    need(pe, on_ready[A], u)
                    need(pe, on_ready[B], u - 2)
                else:
                    need(pe, on_ready[A], capped(u + 3))
                    need(pe, on_ready[B], u)
                for gp in range(2):
                    for hp in range(2):
                        c = 36 * (4 * b + 2 * gp + hp)
                        last = mm(O_bank[:, c:c + 36], PT[n][:, b, 2 * gp + hp], VB[n][:, b, gp, :, hp],
                                  start=True, stop=True)
                last.then_inc(pv_done[n], 1)

            def turn_heads(n, u):
                need(pe, on_ready[n], u + 1)
                if n == A:
                    need(pe, km_ready[A], capped(u + 2))
                    need(pe, km_ready[B], u)
                    need(pe, ot_ready[A], u)
                    need(pe, ot_ready[B], u - 2)
                else:
                    need(pe, km_ready[A], capped(u + 4))
                    need(pe, km_ready[B], capped(u + 2))
                    need(pe, ot_ready[A], capped(u + 3))
                    need(pe, ot_ready[B], u)
                nc.tensor.transpose(K_bank[:, P:2 * P], ON[n][:].rearrange("p m h d -> p (m h d)"), ident[:])\
                    .then_inc(ot_done[n], 1)

            def project_out(n, u):
                pe.wait_ge(rest_in, 16 * REST)
                need(pe, ot_ready[n], u + 1)
                if n == A:
                    need(pe, lg_ready, u - 2)
                    need(pe, xt_ready[A], u)
                else:
                    need(pe, r_ready[A], capped(u + 3))
                    need(pe, xt_ready[A], capped(u + 2))
                    need(pe, lg_ready, u)
                for b in range(2):
                    r = slice(64 * b, 64 * b + 64)
                    for g in range(2):
                        last = mm(Y_bank[r, 0:D], OT[n][r, g], wo[n][r, g], start=(g == 0), stop=(g == 1))
                last.then_inc(y_done[n], 1)

            def turn_x(n, u):
                need(pe, xn_ready[n], u + 1)
                if n == A:
                    need(pe, r_ready[B], u - 1)
                    need(pe, lg_ready, u - 2)
                else:
                    need(pe, xt_ready[A], capped(u + 3))
                nc.tensor.transpose(Y_bank[:, P:2 * P], XN[n][:], ident[:]).then_inc(xt_done[n], 1)

            def route(u):
                need(pe, xt_ready[B], u + 1)
                mm(Y_bank[:, 2 * P:2 * P + E], x2T[:], wr[:], start=True, stop=True).then_inc(lg_done, 1)

            pe.wait_ge(first_in, 16 * FIRST)

            def iteration(ha, hb, ta, tb):
                if ha is not None:
                    project(A, ha)
                if hb is not None:
                    project(B, hb)
                if ha is not None:
                    scores(A, ha, 0)
                if ta is not None:
                    if isinstance(ta, int) and ta == 0:
                        pe.wait_ge(rest_in, 16 * REST)
                    turn_heads(A, ta)
                if hb is not None:
                    scores(B, hb, 0)
                if tb is not None:
                    turn_heads(B, tb)
                if ha is not None:
                    scores(A, ha, 1)
                if ta is not None:
                    project_out(A, ta)
                if ha is not None:
                    turn_probs(A, ha, 0)
                if hb is not None:
                    scores(B, hb, 1)
                if tb is not None:
                    project_out(B, tb)
                if hb is not None:
                    turn_probs(B, hb, 0)
                if ha is not None:
                    weigh_values(A, ha, 0)
                    turn_probs(A, ha, 1)
                if ta is not None:
                    turn_x(A, ta)
                if hb is not None:
                    turn_probs(B, hb, 1)
                if ha is not None:
                    weigh_values(A, ha, 1)
                if tb is not None:
                    turn_x(B, tb)
                if hb is not None:
                    weigh_values(B, hb, 0)
                if tb is not None:
                    route(tb)
                if hb is not None:
                    weigh_values(B, hb, 1)

            def bias_out():
                pe.wait_ge(rest_in, 16 * REST)
                pe.wait_ge(bv_ready, 1)
                pe.wait_ge(zero_ready, 1)
                mm(Y_bank[:, 3 * P:4 * P], bv_cols[:], wo_full[:], start=True, stop=False)
                mm(Y_bank[:, 3 * P:4 * P], ones_row[:], bo_row[:], start=False, stop=True).then_inc(bo_sum, 1)

            pe.wait_ge(zero_ready, 1)
            bias_out()
            pe.wait_ge(bo_ready, 1)
            pipeline(pe, iteration)

            pe.wait_ge(chosen_ready, 1)
            mm(bank[6][:, 0:PAIRS * E], before[:], chosen[:].rearrange("p u e -> p (u e)"), start=True, stop=True)\
                .then_inc(pos_done, 1)
            pe.wait_ge(disp_ready, 1)
            def dispatch(m):
                for k in range(2):
                    need(pe, x2s_ready[k], m + 1)
                    need(pe, buf_ready[k], m)
                    mm(bank[k][:, 0:DSLOT], x2s[k][:], disp[:, bass.ds(2 * m + k, 1)].rearrange("p o e s -> p (o e s)"),
                       start=True, stop=True).then_inc(d_done[k], 1)
            peeled(pe, PAIRS // 2, dispatch)
            for k in range(2):
                pe.wait_ge(buf_ready[k], PAIRS // 2)

            def up(e, k, m):
                pe.wait_ge(w_in[k], 32 * m + 32)
                for j in range(FJ):
                    if not (isinstance(e, int) and e == 0):
                        pe.wait_ge(h_ready_act if j % 2 == 0 else h_ready_dve, 2 * e + (j // 2 + 1) - 2)
                    mm(bank[j][:, 0:ESLOT], w1[k][:, P * j:P * j + P], buf[:, bass.ds(e, 1)].rearrange("p o s -> p (o s)"),
                       start=True, stop=True).then_inc(h_done, 1)

            def down(e, k, m):
                pe.wait_ge(h_ready_act, 2 * e + 2)
                pe.wait_ge(h_ready_dve, 2 * e + 2)
                if not (isinstance(m, int) and m == 0):
                    pe.wait_ge(y_ready[k], m)
                for j in range(FJ):
                    last = mm(bank[4 + k][:, 0:ESLOT], w2[k][:, j], HT[k][:, j], start=(j == 0), stop=(j == FJ - 1))
                last.then_inc(ye_done[k], 1)

            up(0, 0, 0)
            up(1, 1, 0)
            down(0, 0, 0)
            def two_experts(m):
                up(2 * m, 0, m)
                down(2 * m - 1, 1, m - 1)
                up(2 * m + 1, 1, m)
                down(2 * m, 0, m)
            two_experts(1)
            with pe.Fori(2, E // 2) as m:
                two_experts(m)
            down(E - 1, 1, E // 2 - 1)

            def turn_pair(k, m):
                pe.wait_ge(ygin_ready[k], m + 1)
                if not (isinstance(m, int) and m == 0):
                    pe.wait_ge(yg_ready[k], m)
                for n in range(4):
                    last = nc.tensor.transpose(bank[k][0:BSLOT, P * n:P * n + P], yg_in[k][:, n], ident[:])
                last.then_inc(ygt_done[k], 1)

            def combine(k, m):
                pe.wait_ge(yg_ready[k], m + 1)
                need(pe, fr_ready[k], m)
                for b in range(2):
                    last = mm(bank[6 + k][:, 0:D], yg[k][0:BSLOT, 2 + b], yg[k][0:BSLOT, b], start=(b == 0), stop=(b == 1))
                last.then_inc(c_done[k], 1)

            for k in range(2):
                turn_pair(k, 0)
            def pairs(m):
                for k in range(2):
                    combine(k, m - 1)
                    turn_pair(k, m)
            pairs(1)
            with pe.Fori(2, PAIRS // 2) as m:
                pairs(m)
            for k in range(2):
                combine(k, PAIRS // 2 - 1)

        @block.vector
        def _(dve):
            V = nc.vector

            def mask_keys(n, u):
                need(dve, k_done[n], u + 1)
                need(dve, s_done[n], 2 * u)
                src = K_bank[:, 0:P].rearrange("p (b k) -> p b k", b=2)
                if n == A:
                    V.tensor_tensor(KM[n][:], src.unsqueeze(2).broadcast_to([P, 2, 4, SEQ]), headed(hmask[:], 2), ALU.mult)\
                        .then_inc(km_ready[n], 1)
                else:
                    for b in range(2):
                        last = V.scalar_tensor_tensor(KM[n][:, b], headed(src[:, b], 4), bias[:, 1:2], hmask[:],
                                                      ALU.add, ALU.mult)
                    last.then_inc(km_ready[n], 1)

            def row_max(n, u, b):
                need(dve, s_done[n], 2 * u + b + 1)
                V.tensor_reduce(MX[n][:, b], S_bank[n][:].rearrange("p (h k) -> p h k", k=SEQ), AX.X, ALU.max)\
                    .then_inc(mx_ready[n], 1)

            def less_max(n, u, b):
                need(dve, mx_ready[n], 2 * u + b + 1)
                need(dve, t_done[n], 2 * u + b - 1)
                V.tensor_tensor(PZ[n][:, b], S_bank[n][:].rearrange("p (h k) -> p h k", k=SEQ),
                                MX[n][:, b].unsqueeze(2).broadcast_to([P, 8, SEQ]), ALU.subtract).then_inc(z_ready[n], 1)

            def turned_probs(n, u, b):
                need(dve, t_done[n], 2 * u + b + 1)
                need(dve, pv_done[n], 2 * u + b - 1)
                V.tensor_scalar(PT[n][:, b].rearrange("p m q -> p (m q)"), PT_bank[n][:], CLIP_FLOOR, None, ALU.max)\
                    .then_inc(pt_ready[n], 1)

            def normalise(n, u):
                need(dve, pv_done[n], 2 * u + 2)
                need(dve, ot_done[n], u)
                for g in range(2):
                    r = slice(64 * g, 64 * g + 64)
                    den = O_view[r, :, g, :, DH]
                    last = V.tensor_scalar(DEN[n][r], den, SOFTMAX_EPS if n == A else 0.0, None, ALU.add)
                last.then_inc(den_ready[n], 1)
                need(dve, den_ready[n], u + 1)
                V.reciprocal(REC[n][:], DEN[n][:]).then_inc(rec_ready[n], 1)
                need(dve, rec_ready[n], u + 1)
                for g in range(2):
                    r = slice(64 * g, 64 * g + 64)
                    last = V.tensor_tensor(ON[n][r], O_view[r, :, g, :, 0:DH],
                                           REC[n][r].unsqueeze(3).broadcast_to([64, 8, 2, DH]), ALU.mult)
                last.then_inc(on_ready[n], 1)

            def residual(n, u):
                need(dve, y_done[n], u + 1)
                if n == A:
                    x = xnat[:, bass.ds(u, 1)]
                else:
                    need(dve, x1b_ready, u + 1)
                    x = x1b_all[:, bass.ds(u, 1)]
                V.tensor_tensor(R[n][:], Y_bank[:, 0:D], x.rearrange("p o c -> p (o c)"), ALU.add).then_inc(r_ready[n], 1)
                need(dve, r_ready[n], u + 1)
                V.bn_stats(ST[n][:], R[n][:]).then_inc(st_ready[n], 1)
                dve.wait_ge(rest_in, 16 * REST)
                need(dve, st_ready[n], u + 1)
                V.bn_aggr(MV[n][:], ST[n][:]).then_inc(mv_ready[n], 1)
                need(dve, mv_ready[n], u + 1)
                V.tensor_scalar(VE[n][:], MV[n][:, 1:2], LN_EPS, None, ALU.add).then_inc(ve_ready[n], 1)

            def layer_norm(n, u):
                need(dve, rs_ready[n], u + 1)
                need(dve, xt_done[n], u)
                need(dve, x1b_ready if n == A else x2_kept, u)
                V.tensor_scalar(XN[n][:], R[n][:], MV[n][:, 0:1], RS[n][:], ALU.subtract, ALU.mult)\
                    .then_inc(xn_ready[n], 1)

            dve.wait_ge(first_in, 16 * FIRST)
            dve.wait_ge(bo_sum, 1)
            V.tensor_copy(bo_all[:], Y_bank[:, 3 * P:4 * P]).then_inc(bo_ready, 1)

            def iteration(ha, hb, ta, tb):
                if ha is not None:
                    mask_keys(A, ha)
                if hb is not None:
                    mask_keys(B, hb)
                if ha is not None:
                    row_max(A, ha, 0)
                    less_max(A, ha, 0)
                if hb is not None:
                    row_max(B, hb, 0)
                    less_max(B, hb, 0)
                if ha is not None:
                    row_max(A, ha, 1)
                    less_max(A, ha, 1)
                if ta is not None:
                    residual(A, ta)
                if ha is not None:
                    turned_probs(A, ha, 0)
                if hb is not None:
                    row_max(B, hb, 1)
                    less_max(B, hb, 1)
                if ta is not None:
                    layer_norm(A, ta)
                if tb is not None:
                    residual(B, tb)
                if ha is not None:
                    turned_probs(A, ha, 1)
                if tb is not None:
                    layer_norm(B, tb)
                if ha is not None:
                    normalise(A, ha)
                if hb is not None:
                    normalise(B, hb)

            pipeline(dve, iteration)

            count = [0]

            def then(ins):
                count[0] += 1
                ins.then_inc(router, 1)
                dve.wait_ge(router, count[0])

            wide = lambda t: t[:].unsqueeze(2).broadcast_to([P, PAIRS, E])
            dve.wait_ge(lg_ready, PAIRS)
            then(V.tensor_reduce(rmax[:], logits[:], AX.X, ALU.max))
            V.tensor_tensor(rz[:], logits[:], wide(rmax), ALU.subtract).then_inc(rz_ready, 1)
            dve.wait_ge(rexp_ready, 1)
            then(V.tensor_reduce(rmax[:], prob[:], AX.X, ALU.add))
            then(V.reciprocal(rmax[:], rmax[:]))
            then(V.tensor_tensor(prob[:], prob[:], wide(rmax), ALU.mult))
            left = prob
            for k in range(TOPK):
                then(V.tensor_reduce(rmax[:], left[:], AX.X, ALU.max))
                then(V.tensor_tensor(cand[:], left[:], wide(rmax), ALU.is_equal))
                then(V.tensor_tensor(cand[:], cand[:], headed(rank[:], PAIRS), ALU.mult))
                then(V.tensor_reduce(rmax[:], cand[:], AX.X, ALU.max))
                then(V.tensor_tensor(pick[k][:], cand[:], wide(rmax), ALU.is_equal))
                if k == 0:
                    flat = lambda t: t[:].rearrange("p u e -> p (u e)")
                    then(V.scalar_tensor_tensor(flat(rz), flat(pick[0]), -2.0, flat(prob), ALU.mult, ALU.add))
                    left = rz
            V.tensor_tensor(chosen[:], pick[0][:], pick[1][:], ALU.add).then_inc(chosen_ready, 1)
            dve.wait_ge(chosen_ready, 1)
            V.tensor_tensor(gate[:], prob[:], chosen[:], ALU.mult)
            dve.wait_ge(pos_done, 1)
            then(V.scalar_tensor_tensor(flat(place), bank[6][:, 0:PAIRS * E], 1.0, flat(chosen), ALU.add, ALU.mult))
            then(V.tensor_scalar(place[:], place[:], -1.0, None, ALU.add))
            V.tensor_tensor(disp[:].rearrange("p u e s -> p (u e) s"), headed(slotno[:], PAIRS * E),
                            flat(place).unsqueeze(2).broadcast_to([P, PAIRS * E, PSLOT]), ALU.is_equal).then_inc(disp_ready, 1)
            dve.wait_ge(disp_ready, 1)

            bufv = buf[:].rearrange("p e (u s) -> p u e s", s=PSLOT)
            with dve.Fori(0, PAIRS // 2) as m:
                dve.wait_ge(d_done[1], m + 1)
                V.tensor_copy(bufv[:, bass.ds(2 * m + 1, 1)].rearrange("p o e s -> p (o e) s"),
                              bank[1][:, 0:DSLOT].rearrange("p (e s) -> p e s", s=PSLOT)).then_inc(buf_ready[1], 1)
            V.tensor_tensor(gdisp[:].rearrange("p u e s -> p (u e) s"), disp[:].rearrange("p u e s -> p (u e) s"),
                            flat(gate).unsqueeze(2).broadcast_to([P, PAIRS * E, PSLOT]), ALU.mult).then_inc(gdisp_ready, 1)

            def experts(m):
                for k in range(2):
                    e = 2 * m + k
                    for j in (1, 3):
                        dve.wait_ge(h_done, FJ * e + j + 1)
                        if not isinstance(m, int) or m > 0:
                            dve.wait_ge(ye_done[k], m)
                        V.tensor_scalar(HT[k][:, j], bank[j][:, 0:ESLOT], b1[:, bass.ds(e, 1), j], 0.0, ALU.add, ALU.max)\
                            .then_inc(h_ready_dve, 1)
                    if k == 0 and (not isinstance(m, int) or m > 0):
                        odd_result(m - 1)

            def odd_result(m):
                dve.wait_ge(ye_done[1], m + 1)
                V.tensor_scalar(yexp[:, bass.ds(2 * m + 1, 1)].rearrange("p o s -> p (o s)"), bank[5][:, 0:ESLOT],
                                b2[:, bass.ds(2 * m + 1, 1)], None, ALU.add).then_inc(y_ready[1], 1)
            experts(0)
            with dve.Fori(1, E // 2) as m:
                experts(m)
            odd_result(E // 2 - 1)

            def sum_stats(k, m):
                dve.wait_ge(c_done[k], m + 1)
                need(dve, res_ready[k], m)
                V.tensor_tensor(R[k][:], bank[6 + k][:, 0:D], x2_all[:, bass.ds(2 * m + k, 1)].rearrange("p o c -> p (o c)"),
                                ALU.add).then_inc(fr_ready[k], 1)
                dve.wait_ge(fr_ready[k], m + 1)
                V.bn_stats(ST[k][:], R[k][:]).then_inc(fst[k], 1)
                dve.wait_ge(rest_in, 16 * REST)
                dve.wait_ge(fst[k], m + 1)
                V.bn_aggr(MV[k][:], ST[k][:]).then_inc(fmv[k], 1)
                dve.wait_ge(fmv[k], m + 1)
                V.tensor_scalar(VE[k][:], MV[k][:, 1:2], LN_EPS, None, ALU.add).then_inc(fve[k], 1)

            def finish(m):
                for k in range(2):
                    sum_stats(k, m)
                for k in range(2):
                    dve.wait_ge(frs[k], m + 1)
                    need(dve, out_done, 32 * m)
                    V.tensor_scalar(res[k][:], R[k][:], MV[k][:, 0:1], RS[k][:], ALU.subtract, ALU.mult)\
                        .then_inc(res_ready[k], 1)
            peeled(dve, PAIRS // 2, finish)


FIRST = 6
REST = 17


def kernel(x, ctx_1024, L0_attn_Wqkv, L0_attn_Wout, L0_xattn_Wq, L0_xattn_bq, L0_xattn_Wk, L0_xattn_bk, L0_xattn_Wv,
           L0_xattn_bv, L0_xattn_Wo, L0_xattn_bo, L0_ffn_Wr, L0_ffn_W1, L0_ffn_b1, L0_ffn_W2, L0_ffn_b2):
    import concourse.bacc as bacc
    from concourse.bass_utils import run_bass_kernel_spmd

    c = np.ascontiguousarray

    def by_group(w):
        t = np.asarray(w).T.reshape(2, 2, 32, D).transpose(0, 2, 1, 3).reshape(64, 2, D)
        return c(np.concatenate([t, t], axis=0))

    x, ctx_1024 = np.asarray(x), np.asarray(ctx_1024)
    wqkv = np.asarray(L0_attn_Wqkv).T
    row = np.arange(P)
    tok, batch = row % SEQ, row // SEQ
    hh = (row // DH) % 4
    f = np.float32
    slot = np.where(batch[:, None, None] == np.arange(2)[None, :, None], np.arange(CAP)[None, None, :], -2)
    arrays = {
        "xT": c(x.reshape(PAIRS * P, D).T),
        "cT": c(ctx_1024.reshape(PAIRS * P, D).T),
        "xnat": c(x.reshape(PAIRS, P, D).transpose(1, 0, 2)),
        "wq_self": c(wqkv[:, 0:D]), "wk_self": c(wqkv[:, D:2 * D]), "wv_self": c(wqkv[:, 2 * D:3 * D]),
        "wo_self": by_group(L0_attn_Wout),
        "wq_cross": c(np.asarray(L0_xattn_Wq).T), "wk_cross": c(np.asarray(L0_xattn_Wk).T),
        "wv_cross": c(np.asarray(L0_xattn_Wv).T), "wo_cross": by_group(L0_xattn_Wo),
        "wo_full": c(np.asarray(L0_xattn_Wo).T),
        "bias": c(np.stack([np.asarray(b) for b in (L0_xattn_bq, L0_xattn_bk, L0_xattn_bv, L0_xattn_bo)], axis=1)),
        "bo_row": c(np.asarray(L0_xattn_bo)[None, :]),
        "wr": c(np.asarray(L0_ffn_Wr)),
        "w1": c(np.asarray(L0_ffn_W1)), "w2": c(np.asarray(L0_ffn_W2)),
        "b1": c(np.asarray(L0_ffn_b1).reshape(E, FJ, P).transpose(2, 0, 1)),
        "b2": c(np.asarray(L0_ffn_b2).T),
        "ident": np.eye(P, dtype=f),
        "hmask": c(np.broadcast_to((hh[:, None, None] == np.arange(4)[None, :, None]), (P, 4, SEQ)).astype(f)),
        "before": ((tok[:, None] < tok[None, :]) & (batch[:, None] == batch[None, :])).astype(f),
        "rank": c(np.broadcast_to(E - np.arange(E), (P, E)).astype(f)),
        "slotno": c(slot.reshape(P, PSLOT).astype(f)),
    }
    nc = bacc.Bacc("TRN2", target_bir_lowering=False, num_devices=1)
    t_in = {k: nc.dram_tensor(f"in_{k}", v.shape, F32, kind="ExternalInput").ap() for k, v in arrays.items()}
    out = nc.dram_tensor("out", (PAIRS, P, D), F32, kind="ExternalOutput").ap()
    decoder_kernel(nc, t_in, out)
    r = run_bass_kernel_spmd(nc, [{f"in_{k}": v for k, v in arrays.items()}], core_ids=[0])
    return r.results[0]["out"].reshape(BATCH, SEQ, D)
```

```python
from contextlib import ExitStack

import concourse.bass as bass
from concourse import mybir
import numpy as np

F32 = mybir.dt.float32
ALU = mybir.AluOpType
ACT = mybir.ActivationFunctionType
AX = mybir.AxisListType

P = 128
BATCH, SEQ, D = 32, 64, 128
PAIRS = BATCH // 2
HEADS, DH = 16, 8
SCALE = 1.0 / float(np.sqrt(DH))
SOFTMAX_EPS = 1e-6
CLIP_FLOOR = float(np.exp(-50.0))
LN_EPS = 1e-5
E = 8
FF = 512
FJ = FF // P
TOPK = 2
CAP = int(SEQ / E * 1.25)
PSLOT = 2 * CAP
ESLOT = PAIRS * PSLOT
DSLOT = E * PSLOT
BSLOT = E * CAP
A, B = 0, 1
LAGS = 4


def need(eng, sem, count):
    if isinstance(count, int) and count <= 0:
        return
    eng.wait_ge(sem, count)


def peeled(eng, count, body, first=1):
    for m in range(first):
        body(m)
    with eng.Fori(first, count) as m:
        body(m)


def pipeline(eng, iteration):
    def run(i):
        def at(lag, step, *args):
            u = i - lag
            if not isinstance(u, int) or 0 <= u < PAIRS:
                step(*args, u)
        def read(*results):
            for n, (lag, ready) in enumerate(results):
                if n == 0 or isinstance(i, int):
                    need(eng, ready, min(i - lag + 1, PAIRS) if isinstance(i, int) else i - lag + 1)
        iteration(at, read)
    for i in range(LAGS + 1):
        run(i)
    with eng.Fori(LAGS + 1, PAIRS) as i:
        run(i)
    for i in range(PAIRS, PAIRS + LAGS):
        run(i)


def decoder_kernel(nc, t_in, out):
    with ExitStack() as ctx:
        def sb(name, shape):
            return ctx.enter_context(nc.sbuf_tensor(name, shape, F32))

        def sem(name):
            return ctx.enter_context(nc.semaphore(name))

        def sem2(name):
            return [sem(name + "_self"), sem(name + "_cross")]

        xT = sb("xT", [P, PAIRS * P])
        cT = sb("cT", [P, PAIRS * P])
        xnat = sb("xnat", [P, PAIRS, D])
        x1b_all = sb("x1b_all", [P, PAIRS, D])
        x2_all = sb("x2_all", [P, PAIRS, D])
        logits = sb("logits", [P, PAIRS, E])
        self_first = sb("self_first", [P, 3 * D + 4 * SEQ])
        self_rest = sb("self_rest", [P, 2 * P + 2 * 32])
        others = sb("others", [P, sum(n for _, n in OTHERS)])
        bo_row = sb("bo_row", [1, D])
        ones_row = sb("ones_row", [1, P])
        col = dict(zip((name for name, _ in OTHERS), np.cumsum([0] + [n for _, n in OTHERS]).tolist()))
        other = lambda name: others[:, col[name]:col[name] + dict(OTHERS)[name]]
        wq = [self_first[:, 0:D], other("wq")]
        wk = [self_first[:, D:2 * D], other("wk")]
        wv = [self_first[:, 2 * D:3 * D], other("wv")]
        hmask = self_first[:, 3 * D:].rearrange("p (h k) -> p h k", h=4)
        ident = self_rest[:, 0:P]
        wo = [self_rest[:, P:2 * P], other("wo")]
        ones_sel = self_rest[:, 2 * P:].rearrange("p (h j) -> p h j", h=2)
        before, rank, slotno, wr, bias, b2 = [other(name) for name in ("before", "rank", "slotno", "wr", "bias", "b2")]
        b1 = other("b1").rearrange("p (e j) -> p e j", j=FJ)
        bk_masked = sb("bk_masked", [P, 4])
        bv_cols = sb("bv_cols", [P, P])
        bo_all = sb("bo_all", [P, D])
        mhalf = sb("mhalf", [P, 1])
        xs = [sb(f"xs{n}", [P, 2, 2, SEQ]) for n in (A, B)]
        x1T = sb("x1T", [P, 2, SEQ])
        QZ = [sb(f"QZ{n}", [P, 2, 4, SEQ]) for n in (A, B)]
        KM = [sb(f"KM{n}", [P, 2, 4, SEQ]) for n in (A, B)]
        VB = [sb(f"VB{n}", [P, 8, 96]) for n in (A, B)]
        MX = [sb(f"MX{n}", [P, 2, 8]) for n in (A, B)]
        PZ = [sb(f"PZ{n}", [P, 2, 8, SEQ]) for n in (A, B)]
        PT = [sb(f"PT{n}", [P, 2, 4, P]) for n in (A, B)]
        DEN = sb("DEN", [P, P])
        REC = [sb(f"REC{n}", [P, P]) for n in (A, B)]
        ON = [sb(f"ON{n}", [P, P]) for n in (A, B)]
        R = [sb(f"R{n}", [P, D]) for n in (A, B)]
        ST = [sb(f"ST{n}", [P, 6]) for n in (A, B)]
        MV = [sb(f"MV{n}", [P, 2]) for n in (A, B)]
        VE = [sb(f"VE{n}", [P, 1]) for n in (A, B)]
        RS = [sb(f"RS{n}", [P, 1]) for n in (A, B)]
        XN = [sb(f"XN{n}", [P, D]) for n in (A, B)]
        x2T = sb("x2T", [P, P])
        rmax = sb("rmax", [P, PAIRS])
        rz = sb("rz", [P, PAIRS, E])
        prob = sb("prob", [P, PAIRS, E])
        pick = [sb(f"pick{k}", [P, PAIRS, E]) for k in range(TOPK)]
        cand = sb("cand", [P, PAIRS, E])
        chosen = sb("chosen", [P, PAIRS, E])
        gate = sb("gate", [P, PAIRS, E])
        place = sb("place", [P, PAIRS, E])
        disp = sb("disp", [P, PAIRS, 2, E, CAP])
        gdisp = sb("gdisp", [P, PAIRS, 2, E, CAP])
        buf = sb("buf", [P, E, ESLOT])
        yexp = sb("yexp", [P, 2 * PAIRS, E, CAP])
        w1 = sb("w1", [P, E, FF])
        w2 = sb("w2", [P, E, FJ, D])
        HT = [sb(f"HT{n}", [P, FJ, ESLOT]) for n in range(2)]
        yg = [sb(f"yg{n}", [P, 4, P]) for n in range(2)]
        res = [sb(f"res{n}", [P, D]) for n in range(2)]

        bank = [ctx.enter_context(nc.psum_tensor(f"bank{n}", [P, 512], F32)) for n in range(8)]
        S_bank = [bank[0], bank[1]]
        PT_bank = [bank[2], bank[3]]
        Q_bank = [bank[6][:, 2 * P:3 * P], bank[5][:, 0:P]]
        K_bank = [bank[7][:, 0:P], bank[5][:, 0:P]]
        V_bank = [bank[7][:, 0:2 * P], bank[7][:, 0:2 * P]]
        num_bank = [bank[6][:, 0:P], bank[4][:, 0:P]]
        den_bank = [bank[6][:, P:2 * P], bank[4][:, P:2 * P]]
        Y_bank = [bank[5][:, 0:P], bank[7][:, 0:P]]
        XT_bank = [bank[4][:, 2 * P:3 * P], bank[6][:, 2 * P:3 * P]]
        logit_bank = bank[5][:, 0 * P:0 * P + E]

        first_in, rest_in, out_done = sem("first_in"), sem("rest_in"), sem("out_done")
        w_in = sem("w_in")
        zero_ready, bv_ready = sem("zero_ready"), sem("bv_ready")
        bo_sum, bo_ready = sem("bo_sum"), sem("bo_ready")
        xs_ready = sem2("xs_ready")
        q_done, k_done, v_done = sem2("q_done"), sem2("k_done"), sem2("v_done")
        qz_ready, vb_ready, km_ready = sem2("qz_ready"), sem2("vb_ready"), sem2("km_ready")
        s_done, mx_ready, z_ready, p_ready = sem2("s_done"), sem2("mx_ready"), sem2("z_ready"), sem2("p_ready")
        bk_ready = sem("bk_ready")
        t_done, pt_ready, pv_done = sem2("t_done"), sem2("pt_ready"), sem2("pv_done")
        den_ready, rec_ready, on_ready, y_done = sem("den_ready"), sem2("rec_ready"), sem2("on_ready"), sem2("y_done")
        r_ready, st_ready, mv_ready, ve_ready = sem2("r_ready"), sem2("st_ready"), sem2("mv_ready"), sem2("ve_ready")
        rs_ready, xn_ready, xt_done, xt_ready = sem2("rs_ready"), sem2("xn_ready"), sem2("xt_done"), sem2("xt_ready")
        x1b_ready, x2_kept, lg_done, lg_ready = sem("x1b_ready"), sem("x2_kept"), sem("lg_done"), sem("lg_ready")

        ye_done = [sem("ye_done0"), sem("ye_done1")]
        h_done, h_ready_act, h_ready_dve = sem("h_done"), sem("h_ready_act"), sem("h_ready_dve")
        y_ready = [sem("yexp_ready0"), sem("yexp_ready1")]
        d_done = [sem("d_done0"), sem("d_done1")]
        buf_ready = [sem("buf_ready0"), sem("buf_ready1")]
        ygt_done = [sem("ygt_done0"), sem("ygt_done1")]
        yg_ready = [sem("yg_ready0"), sem("yg_ready1")]
        c_done = [sem("c_done0"), sem("c_done1")]
        fr_ready, fst, fmv = [sem("fr0"), sem("fr1")], [sem("fst0"), sem("fst1")], [sem("fmv0"), sem("fmv1")]
        fve, frs, res_ready = [sem("fve0"), sem("fve1")], [sem("frs0"), sem("frs1")], [sem("res0"), sem("res1")]
        router, rz_ready, rexp_ready = sem("router"), sem("rz_ready"), sem("rexp_ready")
        chosen_ready, pos_done, gate_ready, disp_ready, gdisp_ready = sem("chosen_ready"), sem("pos_done"), sem("gate_ready"), sem("disp_ready"), sem("gdisp_ready")

        def headed(ap, n):
            return ap.unsqueeze(1).broadcast_to([ap.shape[0], n, *ap.shape[1:]])

        xt_view = [t[:, :].rearrange("p (u b k) -> p u b k", b=2, k=SEQ) for t in (xT, cT)]

        def by_slot(t):
            return t[:].unsqueeze(3).broadcast_to([P, PAIRS, E, CAP])

        def slots_of(u):
            v = buf[:].rearrange("p e (u b s) -> p u e b s", b=2, s=CAP)
            return v[:, bass.ds(u, 1)].rearrange("p o e b s -> p (o e) b s")

        def dispatched(ps):
            return ps[:, 0:DSLOT].rearrange("p (b e s) -> p e b s", b=2, s=CAP)

        def expert_result(e):
            v = yexp[:].rearrange("p n e s -> p e n s")
            return v[:, bass.ds(e, 1)].rearrange("p o n s -> p (o n) s")

        def result(ps):
            return ps[:, 0:ESLOT].rearrange("p (n s) -> p n s", s=CAP)

        block = ctx.enter_context(nc.Block())

        @block.sync
        def _(sp):
            def load(dst, src, s):
                sp.dma_start(dst, src).then_inc(s, 16)
            start = 2 * P
            load(self_first[:], t_in["self_first"], first_in)
            load(xT[:, 0:start], t_in["xT"][:, 0:start], first_in)
            load(self_rest[:], t_in["self_rest"], rest_in)
            load(xT[:, start:], t_in["xT"][:, start:], rest_in)
            load(cT[:], t_in["cT"], rest_in)
            load(others[:], t_in["others"], rest_in)
            load(bo_row[:], t_in["bo_row"], rest_in)
            load(xnat[:], t_in["xnat"], rest_in)
            sp.dma_start(w1[:], t_in["w1"].rearrange("e c f -> c e f")).then_inc(w_in, 16)
            sp.dma_start(w2[:], t_in["w2"].rearrange("e (j p) c -> p e j c", p=P)).then_inc(w_in, 16)
            with sp.Fori(0, PAIRS // 2) as m:
                for k in range(2):
                    sp.wait_ge(res_ready[k], m + 1)
                    sp.dma_start(out[bass.ds(2 * m + k, 1)].rearrange("o t c -> t (o c)"), res[k][:]).then_inc(out_done, 16)
            sp.wait_ge(out_done, 16 * PAIRS)

        @block.gpsimd
        def _(pool):
            for n in (A, B):
                nc.gpsimd.memset(QZ[n][:], 0.0)
                nc.gpsimd.memset(VB[n][:], 0.0)
            nc.gpsimd.memset(mhalf[:], -0.5)
            nc.gpsimd.memset(ones_row[:], 1.0).then_inc(zero_ready, 1)
            pool.wait_ge(zero_ready, 1)
            def stage(n, u):
                if isinstance(u, int) and u == 0 and n == A:
                    pool.wait_ge(first_in, 16 * FIRST)
                if isinstance(u, int) and u == 1 and n == A:
                    prepare_biases()
                need(pool, k_done[n], u)
                need(pool, v_done[n], u)
                if n == A:
                    need(pool, q_done[A], u)
                src = xt_view[n][:, bass.ds(u, 1)].rearrange("p o b k -> p (o b) k")
                nc.gpsimd.tensor_copy(xs[n][:], src.unsqueeze(2).broadcast_to([P, 2, 2, SEQ])).then_inc(xs_ready[n], 1)

            def power(n, u):
                need(pool, ve_ready[n], u + 1)
                nc.gpsimd.tensor_tensor(RS[n][:], VE[n][:], mhalf[:], ALU.pow).then_inc(rs_ready[n], 1)

            def keep_x1(u):
                need(pool, xn_ready[A], u + 1)
                if isinstance(u, int):
                    pool.wait_ge(bo_ready, 1)
                nc.gpsimd.tensor_tensor(x1b_all[:, bass.ds(u, 1)].rearrange("p o c -> p (o c)"), XN[A][:],
                                        bo_all[:], ALU.add).then_inc(x1b_ready, 1)

            def keep_x2(u):
                need(pool, xn_ready[B], u + 1)
                nc.gpsimd.tensor_copy(x2_all[:, bass.ds(u, 1)].rearrange("p o c -> p (o c)"), XN[B][:])\
                    .then_inc(x2_kept, 1)

            def prepare_biases():
                pool.wait_ge(rest_in, 16 * REST)
                nc.gpsimd.tensor_copy(bv_cols[:], bias[:, 2:3].broadcast_to([P, P])).then_inc(bv_ready, 1)
                nc.gpsimd.tensor_tensor(bk_masked[:], bias[:, 1:2].broadcast_to([P, 4]), hmask[:, :, 0], ALU.mult)\
                    .then_inc(bk_ready, 1)

            def iteration(at, read):
                at(0, stage, A)
                at(2, stage, B)
                at(3, keep_x1)
                at(2, power, A)
                at(4, power, B)
                at(4, keep_x2)

            pipeline(pool, iteration)

            pool.wait_ge(gate_ready, 1)
            pool.wait_ge(disp_ready, 2)
            for b in range(2):
                nc.gpsimd.tensor_tensor(gdisp[:, :, b], disp[:, :, b], by_slot(gate), ALU.mult).then_inc(gdisp_ready, 1)

            def final_power(k, m):
                pool.wait_ge(fve[k], m + 1)
                nc.gpsimd.tensor_tensor(RS[k][:], VE[k][:], mhalf[:], ALU.pow).then_inc(frs[k], 1)
            with pool.Fori(0, PAIRS // 2) as m:
                for k in range(2):
                    final_power(k, m)

        @block.scalar
        def _(act):
            def spread_queries(n, u):
                need(act, q_done[n], u + 1)
                need(act, s_done[n], 2 * u)
                for g in range(4):
                    r = slice(32 * g, 32 * g + 32)
                    src = Q_bank[n][r].rearrange("p (b q) -> p b q", b=2)
                    if n == A:
                        last = nc.scalar.activation(QZ[n][r, :, g], src, ACT.Copy)
                    else:
                        last = nc.scalar.activation(QZ[n][r, :, g], src, ACT.Identity, bias=bias[r, 0:1])
                last.then_inc(qz_ready[n], 1)

            def spread_values(n, u):
                need(act, v_done[n], u + 1)
                need(act, pv_done[n], 2 * u)
                src = V_bank[n].rearrange("p (m g h d) -> p m g h d", g=2, h=2, d=DH)
                dst = VB[n][:].rearrange("p m (h j) -> p m h j", h=2)
                for hl in range(2):
                    r = slice(64 * hl, 64 * hl + 64)
                    last = nc.scalar.activation(dst[r, :, :, DH * hl:DH * hl + DH], src[r, :, :, hl], ACT.Copy)
                last.then_inc(vb_ready[n], 1)

            def mask_keys(n, u):
                need(act, k_done[n], u + 1)
                need(act, s_done[n], 2 * u)
                if isinstance(u, int) and u == 0:
                    act.wait_ge(bk_ready, 1)
                for h in range(4):
                    last = nc.scalar.activation(KM[n][:, :, h], K_bank[n].rearrange("p (b k) -> p b k", b=2), ACT.Identity,
                                                bias=bk_masked[:, h:h + 1], scale=hmask[:, h, 0:1])
                last.then_inc(km_ready[n], 1)

            def exponentials(n, b, u):
                need(act, z_ready[n], 2 * u + b + 1)
                nc.scalar.activation(PZ[n][:, b], PZ[n][:, b], ACT.Exp, scale=SCALE).then_inc(p_ready[n], 1)

            def turned_probs(n, b, u):
                need(act, t_done[n], 2 * u + b + 1)
                need(act, pv_done[n], 2 * u + b - 1)
                nc.scalar.activation(PT[n][:, b].rearrange("p m q -> p (m q)"), PT_bank[n][:], ACT.Copy)\
                    .then_inc(pt_ready[n], 1)

            def turned_x(n, u):
                need(act, xt_done[n], u + 1)
                if n == A:
                    need(act, q_done[B], u)
                    nc.scalar.activation(x1T[:].rearrange("p b q -> p (b q)"), XT_bank[n], ACT.Copy)\
                        .then_inc(xt_ready[n], 1)
                else:
                    need(act, lg_done, u)
                    nc.scalar.activation(x2T[:], XT_bank[n], ACT.Copy).then_inc(xt_ready[n], 1)

            def keep_logits(u):
                need(act, lg_done, u + 1)
                nc.scalar.activation(logits[:, bass.ds(u, 1)].rearrange("p o e -> p (o e)"), logit_bank,
                                     ACT.Copy).then_inc(lg_ready, 1)

            act.wait_ge(zero_ready, 1)

            def iteration(at, read):
                at(0, spread_queries, A)
                at(2, mask_keys, B)
                at(3, turned_probs, B, 0)
                at(2, turned_x, A)
                at(3, exponentials, B, 1)
                at(2, spread_queries, B)
                at(3, turned_probs, B, 1)
                at(0, exponentials, A, 0)
                at(0, spread_values, A)
                at(0, exponentials, A, 1)
                at(4, turned_x, B)
                at(2, spread_values, B)
                at(2, exponentials, B, 0)
                at(4, keep_logits)

            pipeline(act, iteration)

            act.wait_ge(rz_ready, 1)
            nc.scalar.activation(prob[:], rz[:], ACT.Exp).then_inc(rexp_ready, 1)

            with act.Fori(0, PAIRS // 2) as m:
                act.wait_ge(d_done[0], m + 1)
                nc.scalar.activation(slots_of(2 * m), dispatched(bank[0]), ACT.Copy).then_inc(buf_ready[0], 1)

            def hidden(e, k, j, m):
                act.wait_ge(h_done, FJ * e + j + 1)
                if not isinstance(m, int) or m > 0:
                    act.wait_ge(ye_done[k], m)
                nc.scalar.activation(HT[k][:, j], bank[j][:, 0:ESLOT], ACT.Relu,
                                     bias=b1[:, bass.ds(e, 1), j]).then_inc(h_ready_act, 1)
            def experts(m):
                for k in range(2):
                    e = 2 * m + k
                    for j in (0, 2):
                        hidden(e, k, j, m)
                    if k == 0:
                        continue
                    act.wait_ge(ye_done[0], m + 1)
                    nc.scalar.activation(expert_result(2 * m), result(bank[4]),
                                         ACT.Identity, bias=b2[:, bass.ds(2 * m, 1)]).then_inc(y_ready[0], 1)
            experts(0)
            with act.Fori(1, E // 2) as m:
                experts(m)

            def keep_turned(m):
                for k in range(2):
                    act.wait_ge(ygt_done[k], m + 1)
                    need(act, c_done[k], m)
                    nc.scalar.activation(yg[k][0:BSLOT].rearrange("p n c -> p (n c)"), bank[k][0:BSLOT, :], ACT.Copy)\
                        .then_inc(yg_ready[k], 1)
            peeled(act, PAIRS // 2, keep_turned)

        @block.tensor
        def _(pe):
            mm = nc.tensor.matmul

            def project_queries(n, u):
                need(pe, xs_ready[A] if n == A else xt_ready[A], u + 1)
                mm(Q_bank[n], wq[n], xs[A][:, :, 0] if n == A else x1T[:], start=True, stop=True).then_inc(q_done[n], 1)

            def project_keys(n, u):
                need(pe, xs_ready[n], u + 1)
                mm(K_bank[n], wk[n], xs[n][:, :, 0], start=True, stop=True).then_inc(k_done[n], 1)

            def project_values(n, u):
                need(pe, xs_ready[n], u + 1)
                for b in range(2):
                    last = mm(V_bank[n][:, P * b:P * b + P], xs[n][:, b], wv[n], start=True, stop=True)
                last.then_inc(v_done[n], 1)

            def scores(n, b, u):
                need(pe, qz_ready[n], u + 1)
                need(pe, km_ready[n], u + 1)
                need(pe, z_ready[n], 2 * u + b)
                if isinstance(u, int) and u == 0 and n == B and b == 0:
                    pe.wait_ge(bo_ready, 1)
                for gp in range(2):
                    last = mm(S_bank[n][:, 256 * gp:256 * gp + 256], QZ[n][:, b, 2 * gp:2 * gp + 2], KM[n][:, b],
                              start=True, stop=True)
                last.then_inc(s_done[n], 1)

            def turn_probs(n, b, u):
                if isinstance(u, int) and u == 0 and n == A and b == 0:
                    bias_out()
                need(pe, p_ready[n], 2 * u + b + 1)
                need(pe, pt_ready[n], 2 * u + b)
                for m in range(4):
                    last = nc.tensor.transpose(PT_bank[n][:, P * m:P * m + P], PZ[n][:, b, 2 * m:2 * m + 2].rearrange("p h k -> p (h k)"), ident)
                last.then_inc(t_done[n], 1)

            def weigh_values(n, b, u):
                need(pe, pt_ready[n], 2 * u + b + 1)
                need(pe, vb_ready[n], u + 1)
                for out_bank, sums in ((num_bank, False), (den_bank, True)):
                    for hp in range(2):
                        for g in range(4):
                            w = ones_sel[:, hp] if sums else VB[n][:, 4 * b + g, 32 * hp:32 * hp + 32]
                            q = SEQ * (g % 2)
                            last = mm(out_bank[n][32 * g:32 * g + 32, SEQ * b:SEQ * b + SEQ], w,
                                      PT[n][:, b, 2 * (g // 2) + hp, q:q + SEQ], start=(hp == 0), stop=(hp == 1))
                last.then_inc(pv_done[n], 1)

            def project_out(n, u):
                need(pe, on_ready[n], u + 1)
                mm(Y_bank[n], ON[n][:], wo[n], start=True, stop=True).then_inc(y_done[n], 1)

            def turn_x(n, u):
                need(pe, xn_ready[n], u + 1)
                nc.tensor.transpose(XT_bank[n], XN[n][:], ident).then_inc(xt_done[n], 1)

            def route(u):
                need(pe, xt_ready[B], u + 1)
                mm(logit_bank, x2T[:], wr, start=True, stop=True).then_inc(lg_done, 1)

            pe.wait_ge(first_in, 16 * FIRST)

            def bias_out():
                pe.wait_ge(rest_in, 16 * REST)
                pe.wait_ge(bv_ready, 1)
                pe.wait_ge(zero_ready, 1)
                mm(S_bank[B][:, 0:D], bv_cols[:], wo[B], start=True, stop=False)
                mm(S_bank[B][:, 0:D], ones_row[:], bo_row[:], start=False, stop=True).then_inc(bo_sum, 1)

            def iteration(at, read):
                read((5, xt_ready[B]), (2, on_ready[A]), (1, qz_ready[A]))
                at(0, project_queries, A)
                read((3, vb_ready[B]), (1, vb_ready[A]), (5, r_ready[B]), (1, km_ready[A]))
                at(0, project_keys, A)
                at(3, scores, B, 1)
                read((5, lg_ready), (2, r_ready[A]), (3, qz_ready[B]), (3, km_ready[B]))
                at(2, project_keys, B)
                at(3, turn_probs, B, 0)
                at(1, turn_probs, A, 1)
                at(0, scores, A, 0)
                read((0, qz_ready[A]), (5, xt_ready[B]), (2, on_ready[A]))
                at(1, weigh_values, A, 0)
                read((0, km_ready[A]), (3, vb_ready[B]), (1, vb_ready[A]), (5, r_ready[B]))
                at(4, project_out, B)
                read((4, on_ready[B]), (3, xt_ready[A]))
                at(2, turn_x, A)
                read((0, qz_ready[A]), (5, xt_ready[B]), (2, on_ready[A]))
                at(1, weigh_values, A, 1)
                read((2, km_ready[B]), (5, lg_ready), (2, r_ready[A]), (3, qz_ready[B]))
                at(2, project_queries, B)
                read((2, xt_ready[A]), (4, on_ready[B]))
                at(3, weigh_values, B, 0)
                at(0, scores, A, 1)
                at(3, turn_probs, B, 1)
                read((4, r_ready[B]), (0, km_ready[A]), (3, vb_ready[B]), (1, vb_ready[A]))
                at(0, project_values, A)
                at(2, scores, B, 0)
                read((2, qz_ready[B]), (2, km_ready[B]), (5, lg_ready), (2, r_ready[A]))
                at(1, project_out, A)
                read((2, xt_ready[A]), (4, on_ready[B]))
                at(3, weigh_values, B, 1)
                read((1, on_ready[A]), (0, qz_ready[A]), (5, xt_ready[B]))
                at(4, turn_x, B)
                read((0, vb_ready[A]), (4, r_ready[B]), (0, km_ready[A]), (3, vb_ready[B]))
                at(2, project_values, B)
                at(0, turn_probs, A, 0)
                read((1, r_ready[A]), (2, qz_ready[B]), (2, km_ready[B]), (5, lg_ready))
                at(4, route)

            pipeline(pe, iteration)

            pe.wait_ge(chosen_ready, 1)
            mm(bank[6][:, 0:PAIRS * E], before, chosen[:].rearrange("p u e -> p (u e)"), start=True, stop=True)\
                .then_inc(pos_done, 1)
            pe.wait_ge(disp_ready, 2)
            pe.wait_ge(x2_kept, PAIRS)
            for p in range(PAIRS):
                need(pe, buf_ready[p % 2], p // 2)
                mm(bank[p % 2][:, 0:DSLOT], x2_all[:, p], disp[:, p].rearrange("p b e s -> p (b e s)"),
                   start=True, stop=True).then_inc(d_done[p % 2], 1)
            for k in range(2):
                pe.wait_ge(buf_ready[k], PAIRS // 2)
            pe.wait_ge(w_in, 32)

            def up(e):
                for j in range(FJ):
                    need(pe, h_ready_act if j % 2 == 0 else h_ready_dve, 2 * (e - 1) + j // 2 + 1)
                    mm(bank[j][:, 0:ESLOT], w1[:, e, P * j:P * j + P], buf[:, e], start=True, stop=True)\
                        .then_inc(h_done, 1)

            def down(e):
                pe.wait_ge(h_ready_act, 2 * e + 2)
                pe.wait_ge(h_ready_dve, 2 * e + 2)
                need(pe, y_ready[e % 2], e // 2)
                for j in range(FJ):
                    last = mm(bank[4 + e % 2][:, 0:ESLOT], w2[:, e, j], HT[e % 2][:, j], start=(j == 0), stop=(j == FJ - 1))
                last.then_inc(ye_done[e % 2], 1)

            up(0)
            for e in range(1, E):
                up(e)
                down(e - 1)
            down(E - 1)

            pe.wait_ge(gdisp_ready, 2)
            for k in range(2):
                pe.wait_ge(y_ready[k], E // 2)

            def turn_pair(p):
                k = p % 2
                need(pe, yg_ready[k], p // 2)
                for b in range(2):
                    nc.tensor.transpose(bank[k][0:BSLOT, P * b:P * b + P], yexp[:, 2 * p + b].rearrange("p e s -> p (e s)"), ident)
                    last = nc.tensor.transpose(bank[k][0:BSLOT, P * (2 + b):P * (3 + b)],
                                               gdisp[:, p, b].rearrange("p e s -> p (e s)"), ident)
                last.then_inc(ygt_done[k], 1)

            def combine(p):
                k = p % 2
                pe.wait_ge(yg_ready[k], p // 2 + 1)
                need(pe, fr_ready[k], p // 2)
                for b in range(2):
                    last = mm(bank[6 + k][:, 0:D], yg[k][0:BSLOT, 2 + b], yg[k][0:BSLOT, b], start=(b == 0), stop=(b == 1))
                last.then_inc(c_done[k], 1)

            turn_pair(0)
            for p in range(1, PAIRS):
                turn_pair(p)
                combine(p - 1)
            combine(PAIRS - 1)

        @block.vector
        def _(dve):
            V = nc.vector

            def mask_keys(n, u):
                need(dve, k_done[n], u + 1)
                need(dve, s_done[n], 2 * u)
                src = K_bank[n].rearrange("p (b k) -> p b k", b=2)
                V.tensor_tensor(KM[n][:], src.unsqueeze(2).broadcast_to([P, 2, 4, SEQ]), headed(hmask, 2), ALU.mult)\
                    .then_inc(km_ready[n], 1)

            def row_max(n, b, u):
                need(dve, s_done[n], 2 * u + b + 1)
                V.tensor_reduce(MX[n][:, b], S_bank[n][:].rearrange("p (h k) -> p h k", k=SEQ), AX.X, ALU.max)\
                    .then_inc(mx_ready[n], 1)

            def less_max(n, b, u):
                need(dve, mx_ready[n], 2 * u + b + 1)
                need(dve, t_done[n], 2 * u + b - 1)
                V.tensor_tensor(PZ[n][:, b], S_bank[n][:].rearrange("p (h k) -> p h k", k=SEQ),
                                MX[n][:, b].unsqueeze(2).broadcast_to([P, 8, SEQ]), ALU.subtract).then_inc(z_ready[n], 1)

            def turned_floored(b, u):
                need(dve, t_done[A], 2 * u + b + 1)
                need(dve, pv_done[A], 2 * u + b - 1)
                V.tensor_scalar(PT[A][:, b].rearrange("p m q -> p (m q)"), PT_bank[A][:], CLIP_FLOOR, None, ALU.max)\
                    .then_inc(pt_ready[A], 1)

            def add_eps(u):
                need(dve, pv_done[A], 2 * u + 2)
                V.tensor_scalar(DEN[:], den_bank[A], SOFTMAX_EPS, None, ALU.add).then_inc(den_ready, 1)

            def invert(n, u):
                if n == A:
                    need(dve, den_ready, u + 1)
                else:
                    need(dve, pv_done[B], 2 * u + 2)
                V.reciprocal(REC[n][:], DEN[:] if n == A else den_bank[B]).then_inc(rec_ready[n], 1)

            def normalise(n, u):
                need(dve, rec_ready[n], u + 1)
                need(dve, y_done[n], u)
                V.tensor_tensor(ON[n][:], num_bank[n], REC[n][:], ALU.mult).then_inc(on_ready[n], 1)

            def residual(n, u):
                if isinstance(u, int) and u == 0 and n == A:
                    dve.wait_ge(rest_in, 16 * REST)
                    dve.wait_ge(bo_sum, 1)
                    V.tensor_copy(bo_all[:], S_bank[B][:, 0:D]).then_inc(bo_ready, 1)
                need(dve, y_done[n], u + 1)
                if n == A:
                    x = xnat[:, bass.ds(u, 1)]
                else:
                    need(dve, x1b_ready, u + 1)
                    x = x1b_all[:, bass.ds(u, 1)]
                V.tensor_tensor(R[n][:], Y_bank[n], x.rearrange("p o c -> p (o c)"), ALU.add).then_inc(r_ready[n], 1)

            def statistics(n, u):
                need(dve, r_ready[n], u + 1)
                V.bn_stats(ST[n][:], R[n][:]).then_inc(st_ready[n], 1)

            def mean_variance(n, u):
                dve.wait_ge(rest_in, 16 * REST)
                need(dve, st_ready[n], u + 1)
                V.bn_aggr(MV[n][:], ST[n][:]).then_inc(mv_ready[n], 1)

            def variance_eps(n, u):
                need(dve, mv_ready[n], u + 1)
                V.tensor_scalar(VE[n][:], MV[n][:, 1:2], LN_EPS, None, ALU.add).then_inc(ve_ready[n], 1)

            def layer_norm(n, u):
                need(dve, rs_ready[n], u + 1)
                need(dve, xt_done[n], u)
                need(dve, x1b_ready if n == A else x2_kept, u)
                V.tensor_scalar(XN[n][:], R[n][:], MV[n][:, 0:1], RS[n][:], ALU.subtract, ALU.mult)\
                    .then_inc(xn_ready[n], 1)

            dve.wait_ge(first_in, 16 * FIRST)

            def iteration(at, read):
                at(3, less_max, B, 0)
                at(2, statistics, A)
                at(4, invert, B)
                at(1, turned_floored, 0)
                at(0, mask_keys, A)
                at(2, mean_variance, A)
                at(4, normalise, B)
                at(2, variance_eps, A)
                at(3, row_max, B, 1)
                at(1, turned_floored, 1)
                at(2, layer_norm, A)
                at(0, row_max, A, 0)
                at(3, less_max, B, 1)
                at(4, residual, B)
                at(0, less_max, A, 0)
                at(4, statistics, B)
                at(1, add_eps)
                at(4, mean_variance, B)
                at(1, invert, A)
                at(4, variance_eps, B)
                at(0, row_max, A, 1)
                at(1, normalise, A)
                at(0, less_max, A, 1)
                at(4, layer_norm, B)
                at(2, row_max, B, 0)
                at(1, residual, A)

            pipeline(dve, iteration)

            count = [0]

            def then(ins):
                count[0] += 1
                ins.then_inc(router, 1)
                dve.wait_ge(router, count[0])

            wide = lambda t: t[:].unsqueeze(2).broadcast_to([P, PAIRS, E])
            dve.wait_ge(lg_ready, PAIRS)
            then(V.tensor_reduce(rmax[:], logits[:], AX.X, ALU.max))
            V.tensor_tensor(rz[:], logits[:], wide(rmax), ALU.subtract).then_inc(rz_ready, 1)
            dve.wait_ge(rexp_ready, 1)
            then(V.tensor_reduce(rmax[:], prob[:], AX.X, ALU.add))
            then(V.reciprocal(rmax[:], rmax[:]))
            then(V.tensor_tensor(prob[:], prob[:], wide(rmax), ALU.mult))
            left = prob
            for k in range(TOPK):
                then(V.tensor_reduce(rmax[:], left[:], AX.X, ALU.max))
                then(V.tensor_tensor(cand[:], left[:], wide(rmax), ALU.is_equal))
                then(V.tensor_tensor(cand[:], cand[:], headed(rank, PAIRS), ALU.mult))
                then(V.tensor_reduce(rmax[:], cand[:], AX.X, ALU.max))
                then(V.tensor_tensor(pick[k][:], cand[:], wide(rmax), ALU.is_equal))
                if k == 0:
                    flat = lambda t: t[:].rearrange("p u e -> p (u e)")
                    then(V.scalar_tensor_tensor(flat(rz), flat(pick[0]), -2.0, flat(prob), ALU.mult, ALU.add))
                    left = rz
            V.tensor_tensor(chosen[:], pick[0][:], pick[1][:], ALU.add).then_inc(chosen_ready, 1)
            dve.wait_ge(chosen_ready, 1)
            V.tensor_tensor(gate[:], prob[:], chosen[:], ALU.mult).then_inc(gate_ready, 1)
            dve.wait_ge(pos_done, 1)
            then(V.scalar_tensor_tensor(flat(place), bank[6][:, 0:PAIRS * E], 1.0, flat(chosen), ALU.add, ALU.mult))
            then(V.tensor_scalar(place[:], place[:], -1.0, None, ALU.add))
            for b in range(2):
                V.tensor_tensor(disp[:, :, b], slotno[:, CAP * b:CAP * b + CAP].unsqueeze(1).unsqueeze(1).broadcast_to([P, PAIRS, E, CAP]),
                                by_slot(place), ALU.is_equal).then_inc(disp_ready, 1)

            with dve.Fori(0, PAIRS // 2) as m:
                dve.wait_ge(d_done[1], m + 1)
                V.tensor_copy(slots_of(2 * m + 1), dispatched(bank[1])).then_inc(buf_ready[1], 1)

            def experts(m):
                for k in range(2):
                    e = 2 * m + k
                    for j in (1, 3):
                        dve.wait_ge(h_done, FJ * e + j + 1)
                        if not isinstance(m, int) or m > 0:
                            dve.wait_ge(ye_done[k], m)
                        V.tensor_scalar(HT[k][:, j], bank[j][:, 0:ESLOT], b1[:, bass.ds(e, 1), j], 0.0, ALU.add, ALU.max)\
                            .then_inc(h_ready_dve, 1)
                    if k == 0 and (not isinstance(m, int) or m > 0):
                        odd_result(m - 1)

            def odd_result(m):
                dve.wait_ge(ye_done[1], m + 1)
                V.tensor_scalar(expert_result(2 * m + 1), result(bank[5]),
                                b2[:, bass.ds(2 * m + 1, 1)], None, ALU.add).then_inc(y_ready[1], 1)
            experts(0)
            with dve.Fori(1, E // 2) as m:
                experts(m)
            odd_result(E // 2 - 1)

            def sum_stats(k, m):
                dve.wait_ge(c_done[k], m + 1)
                need(dve, res_ready[k], m)
                V.tensor_tensor(R[k][:], bank[6 + k][:, 0:D], x2_all[:, bass.ds(2 * m + k, 1)].rearrange("p o c -> p (o c)"),
                                ALU.add).then_inc(fr_ready[k], 1)
                dve.wait_ge(fr_ready[k], m + 1)
                V.bn_stats(ST[k][:], R[k][:]).then_inc(fst[k], 1)
                dve.wait_ge(rest_in, 16 * REST)
                dve.wait_ge(fst[k], m + 1)
                V.bn_aggr(MV[k][:], ST[k][:]).then_inc(fmv[k], 1)
                dve.wait_ge(fmv[k], m + 1)
                V.tensor_scalar(VE[k][:], MV[k][:, 1:2], LN_EPS, None, ALU.add).then_inc(fve[k], 1)

            def finish(m):
                for k in range(2):
                    sum_stats(k, m)
                for k in range(2):
                    dve.wait_ge(frs[k], m + 1)
                    need(dve, out_done, 32 * m)
                    V.tensor_scalar(res[k][:], R[k][:], MV[k][:, 0:1], RS[k][:], ALU.subtract, ALU.mult)\
                        .then_inc(res_ready[k], 1)
            peeled(dve, PAIRS // 2, finish)


FIRST, REST = 2, 6
OTHERS = (("wq", D), ("wk", D), ("wv", D), ("wo", D), ("before", P), ("wr", E), ("b1", E * FJ), ("b2", E), ("bias", 4),
          ("rank", E), ("slotno", PSLOT))


def kernel(x, ctx_1024, L0_attn_Wqkv, L0_attn_Wout, L0_xattn_Wq, L0_xattn_bq, L0_xattn_Wk, L0_xattn_bk, L0_xattn_Wv,
           L0_xattn_bv, L0_xattn_Wo, L0_xattn_bo, L0_ffn_Wr, L0_ffn_W1, L0_ffn_b1, L0_ffn_W2, L0_ffn_b2):
    import concourse.bacc as bacc
    from concourse.bass_utils import run_bass_kernel_spmd

    c = np.ascontiguousarray

    x, ctx_1024 = np.asarray(x), np.asarray(ctx_1024)
    wqkv = np.asarray(L0_attn_Wqkv).T
    row = np.arange(P)
    tok, batch = row % SEQ, row // SEQ
    hh = (row // DH) % 4
    f = np.float32
    slot = np.where(batch[:, None, None] == np.arange(2)[None, :, None], np.arange(CAP)[None, None, :], -2)
    heads = np.broadcast_to((hh[:, None, None] == np.arange(4)[None, :, None]), (P, 4, SEQ)).reshape(P, -1).astype(f)
    sums = np.broadcast_to((np.arange(4)[None, None, :, None] == 2 * np.arange(2)[None, :, None, None]
                            + batch[:, None, None, None]), (P, 2, 4, DH)).reshape(P, -1).astype(f)
    small = {
        "wq": np.asarray(L0_xattn_Wq).T, "wk": np.asarray(L0_xattn_Wk).T,
        "wv": np.asarray(L0_xattn_Wv).T, "wo": np.asarray(L0_xattn_Wo).T,
        "bias": np.stack([np.asarray(b) for b in (L0_xattn_bq, L0_xattn_bk, L0_xattn_bv, L0_xattn_bo)], axis=1),
        "wr": np.asarray(L0_ffn_Wr),
        "b1": np.asarray(L0_ffn_b1).reshape(E, FJ, P).transpose(2, 0, 1),
        "b2": np.asarray(L0_ffn_b2).T,
        "before": ((tok[:, None] < tok[None, :]) & (batch[:, None] == batch[None, :])).astype(f),
        "rank": np.broadcast_to(E - np.arange(E), (P, E)).astype(f),
        "slotno": slot.reshape(P, PSLOT).astype(f),
    }
    arrays = {
        "xT": c(x.reshape(PAIRS * P, D).T),
        "cT": c(ctx_1024.reshape(PAIRS * P, D).T),
        "xnat": c(x.reshape(PAIRS, P, D).transpose(1, 0, 2)),
        "self_first": c(np.concatenate([wqkv[:, 0:3 * D], heads], axis=1)),
        "self_rest": c(np.concatenate([np.eye(P, dtype=f), np.asarray(L0_attn_Wout).T, sums], axis=1)),
        "others": c(np.concatenate([small[name].reshape(P, n) for name, n in OTHERS], axis=1)),
        "bo_row": c(np.asarray(L0_xattn_bo)[None, :]),
        "w1": c(np.asarray(L0_ffn_W1)), "w2": c(np.asarray(L0_ffn_W2)),
    }
    nc = bacc.Bacc("TRN2", target_bir_lowering=False, num_devices=1)
    t_in = {k: nc.dram_tensor(f"in_{k}", v.shape, F32, kind="ExternalInput").ap() for k, v in arrays.items()}
    out = nc.dram_tensor("out", (PAIRS, P, D), F32, kind="ExternalOutput").ap()
    decoder_kernel(nc, t_in, out)
    r = run_bass_kernel_spmd(nc, [{f"in_{k}": v for k, v in arrays.items()}], core_ids=[0])
    return r.results[0]["out"].reshape(BATCH, SEQ, D)
```

```python
from contextlib import ExitStack

import concourse.bass as bass
from concourse import mybir
import numpy as np

F32 = mybir.dt.float32
ALU = mybir.AluOpType
ACT = mybir.ActivationFunctionType
AX = mybir.AxisListType

P = 128
BATCH, SEQ, D = 32, 64, 128
PAIRS = BATCH // 2
HEADS, DH = 16, 8
SCALE = 1.0 / float(np.sqrt(DH))
SOFTMAX_EPS = 1e-6
CLIP_FLOOR = float(np.exp(-50.0))
LN_EPS = 1e-5
E = 8
FF = 512
FJ = FF // P
TOPK = 2
CAP = int(SEQ / E * 1.25)
PSLOT = 2 * CAP
ESLOT = PAIRS * PSLOT
DSLOT = E * PSLOT
HALF = PAIRS // 2
HSLOT = HALF * PSLOT
BSLOT = E * CAP
A, B = 0, 1
LAGS = 4


def need(eng, sem, count):
    if isinstance(count, int) and count <= 0:
        return
    eng.wait_ge(sem, count)


def peeled(eng, count, body, first=1):
    for m in range(first):
        body(m)
    with eng.Fori(first, count) as m:
        body(m)


def pipeline(eng, iteration):
    def run(i):
        def at(lag, step, *args):
            u = i - lag
            if not isinstance(u, int) or 0 <= u < PAIRS:
                step(*args, u)
        def read(*results):
            for n, (lag, ready) in enumerate(results):
                if n == 0 or isinstance(i, int):
                    need(eng, ready, min(i - lag + 1, PAIRS) if isinstance(i, int) else i - lag + 1)
        def once(j, step, *args):
            if isinstance(i, int) and i == j:
                step(*args)
        iteration(at, read, once)
    for i in range(LAGS + 1):
        run(i)
    with eng.Fori(LAGS + 1, PAIRS) as i:
        run(i)
    for i in range(PAIRS, PAIRS + LAGS):
        run(i)


def decoder_kernel(nc, t_in, out):
    with ExitStack() as ctx:
        def sb(name, shape):
            return ctx.enter_context(nc.sbuf_tensor(name, shape, F32))

        def sem(name):
            return ctx.enter_context(nc.semaphore(name))

        def sem2(name):
            return [sem(name + "_self"), sem(name + "_cross")]

        xT = sb("xT", [P, PAIRS * P])
        cT = sb("cT", [P, PAIRS * P])
        xnat = sb("xnat", [P, PAIRS, D])
        x1b_all = sb("x1b_all", [P, PAIRS, D])
        x2_all = sb("x2_all", [P, PAIRS, D])
        logits = sb("logits", [P, PAIRS, E])
        self_first = sb("self_first", [P, 3 * D + 4 * SEQ])
        self_rest = sb("self_rest", [P, 2 * P + 2 * 32])
        others = sb("others", [P, sum(n for _, n in OTHERS)])
        bo_row = sb("bo_row", [1, D])
        ones_row = sb("ones_row", [1, P])
        col = dict(zip((name for name, _ in OTHERS), np.cumsum([0] + [n for _, n in OTHERS]).tolist()))
        other = lambda name: others[:, col[name]:col[name] + dict(OTHERS)[name]]
        wq = [self_first[:, 0:D], other("wq")]
        wk = [self_first[:, D:2 * D], other("wk")]
        wv = [self_first[:, 2 * D:3 * D], other("wv")]
        hmask = self_first[:, 3 * D:].rearrange("p (h k) -> p h k", h=4)
        ident = self_rest[:, 0:P]
        wo = [self_rest[:, P:2 * P], other("wo")]
        ones_sel = self_rest[:, 2 * P:].rearrange("p (h j) -> p h j", h=2)
        before, rank, slotno, wr, bias, b2 = [other(name) for name in ("before", "rank", "slotno", "wr", "bias", "b2")]
        b1 = other("b1").rearrange("p (e j) -> p e j", j=FJ)
        bk_masked = sb("bk_masked", [P, 4])
        bv_cols = sb("bv_cols", [P, P])
        bo_all = sb("bo_all", [P, D])
        mhalf = sb("mhalf", [P, 1])
        xs = [sb(f"xs{n}", [P, 2, 2, SEQ]) for n in (A, B)]
        x1T = sb("x1T", [P, 2, SEQ])
        QZ = [sb(f"QZ{n}", [P, 2, 4, SEQ]) for n in (A, B)]
        KM = [sb(f"KM{n}", [P, 2, 4, SEQ]) for n in (A, B)]
        VB = [sb(f"VB{n}", [P, 8, 96]) for n in (A, B)]
        MX = [sb(f"MX{n}", [P, 2, 8]) for n in (A, B)]
        PZ = [sb(f"PZ{n}", [P, 2, 8, SEQ]) for n in (A, B)]
        PT = [sb(f"PT{n}", [P, 2, 4, P]) for n in (A, B)]
        DEN = sb("DEN", [P, P])
        REC = [sb(f"REC{n}", [P, P]) for n in (A, B)]
        ON = [sb(f"ON{n}", [P, P]) for n in (A, B)]
        R = [sb(f"R{n}", [P, D]) for n in (A, B)]
        ST = [sb(f"ST{n}", [P, 6]) for n in (A, B)]
        MV = [sb(f"MV{n}", [P, 2]) for n in (A, B)]
        VE = [sb(f"VE{n}", [P, 1]) for n in (A, B)]
        RS = [sb(f"RS{n}", [P, 1]) for n in (A, B)]
        XN = [sb(f"XN{n}", [P, D]) for n in (A, B)]
        x2T = sb("x2T", [P, P])
        rmax = sb("rmax", [P, PAIRS])
        rz = sb("rz", [P, PAIRS, E])
        prob = sb("prob", [P, PAIRS, E])
        pick = [sb(f"pick{k}", [P, PAIRS, E]) for k in range(TOPK)]
        cand = sb("cand", [P, PAIRS, E])
        chosen = sb("chosen", [P, PAIRS, E])
        gate = sb("gate", [P, PAIRS, E])
        place = sb("place", [P, PAIRS, E])
        disp = sb("disp", [P, PAIRS, 2, E, CAP])
        gdisp = sb("gdisp", [P, PAIRS, 2, E, CAP])
        buf = sb("buf", [P, E, ESLOT])
        yexp = sb("yexp", [P, 2 * PAIRS, E, CAP])
        w1 = sb("w1", [P, E, FF])
        w2 = sb("w2", [P, E, FJ, D])
        HT = [sb(f"HT{n}", [P, FJ, HSLOT]) for n in range(2)]
        yg = [sb(f"yg{n}", [P, 4, P]) for n in range(2)]
        res = [sb(f"res{n}", [P, 2, D]) for n in range(2)]
        total = [sb(f"total{n}", [P, D]) for n in range(4)]

        bank = [ctx.enter_context(nc.psum_tensor(f"bank{n}", [P, 512], F32)) for n in range(8)]
        S_bank = [bank[0], bank[1]]
        PT_bank = [bank[2], bank[3]]
        Q_bank = [bank[6][:, 0:P], bank[5][:, 0:P]]
        K_bank = [bank[4][:, 2 * P:3 * P], bank[5][:, 0:P]]
        V_bank = [bank[6][:, 0:2 * P], bank[6][:, 0:2 * P]]
        num_bank = [bank[4][:, 0:P], bank[7][:, 0:P]]
        den_bank = [bank[4][:, P:2 * P], bank[7][:, P:2 * P]]
        Y_bank = [bank[5][:, 0:P], bank[7][:, 2 * P:3 * P]]
        XT_bank = [bank[5][:, 0:P], bank[4][:, 2 * P:3 * P]]
        logit_bank = bank[4][:, 2 * P:2 * P + E]

        first_in, rest_in, out_done = sem("first_in"), sem("rest_in"), [sem("out_done0"), sem("out_done1")]
        w_in = sem("w_in")
        zero_ready, bv_ready = sem("zero_ready"), sem("bv_ready")
        bo_sum, bo_ready = sem("bo_sum"), sem("bo_ready")
        xs_ready = sem2("xs_ready")
        q_done, k_done, v_done = sem2("q_done"), sem2("k_done"), sem2("v_done")
        qz_ready, vb_ready, km_ready = sem2("qz_ready"), sem2("vb_ready"), sem2("km_ready")
        s_done, mx_ready, z_ready, p_ready = sem2("s_done"), sem2("mx_ready"), sem2("z_ready"), sem2("p_ready")
        e_ready, bk_ready = [sem("e_ready0"), sem("e_ready1")], sem("bk_ready")
        t_done, pt_ready, num_done = sem2("t_done"), sem2("pt_ready"), sem2("num_done")
        den_done, eps_added = sem2("den_done"), sem("eps_added")
        rec_ready, on_ready, y_done = sem2("rec_ready"), sem2("on_ready"), sem2("y_done")
        r_ready, st_ready, mv_ready, ve_ready = sem2("r_ready"), sem2("st_ready"), sem2("mv_ready"), sem2("ve_ready")
        rs_ready, xn_ready, xt_done, xt_ready = sem2("rs_ready"), sem2("xn_ready"), sem2("xt_done"), sem2("xt_ready")
        x1b_ready, x2_kept, lg_done, lg_ready = sem("x1b_ready"), sem("x2_kept"), sem("lg_done"), sem("lg_ready")

        ye_done = [sem("ye_done0"), sem("ye_done1")]
        h_done, h_ready_act, h_ready_dve, y_ready = sem("h_done"), sem("h_ready_act"), sem("h_ready_dve"), sem("y_ready")
        d_done, buf_ready = sem("d_done"), sem("buf_ready")
        ygt_done, yg_ready, c_done = sem("ygt_done"), sem("yg_ready"), sem("c_done")
        fr_ready, fst, fmv, fve, frs = sem("fr_ready"), sem("fst"), sem("fmv"), sem("fve"), sem("frs")
        res_ready = sem("res_ready")
        router, rz_ready, rexp_ready = sem("router"), sem("rz_ready"), sem("rexp_ready")
        chosen_ready, pos_done, gate_ready, disp_ready, gdisp_ready = sem("chosen_ready"), sem("pos_done"), sem("gate_ready"), sem("disp_ready"), sem("gdisp_ready")

        def headed(ap, n):
            return ap.unsqueeze(1).broadcast_to([ap.shape[0], n, *ap.shape[1:]])

        xt_view = [t[:, :].rearrange("p (u b k) -> p u b k", b=2, k=SEQ) for t in (xT, cT)]

        def half(t, h):
            return t[:, HALF * h:HALF * h + HALF]

        def by_slot(t, h):
            return half(t, h).unsqueeze(3).broadcast_to([P, HALF, E, CAP])

        def slots_of(u):
            v = buf[:].rearrange("p e (u b s) -> p u e b s", b=2, s=CAP)
            return v[:, bass.ds(u, 1)].rearrange("p o e b s -> p (o e) b s")

        def dispatched(ps):
            return ps[:, 0:DSLOT].rearrange("p (b e s) -> p e b s", b=2, s=CAP)

        def expert_result(h, e):
            v = yexp[:, 2 * HALF * h:2 * HALF * (h + 1)].rearrange("p n e s -> p e n s")
            return v[:, bass.ds(e, 1)].rearrange("p o n s -> p (o n) s")

        block = ctx.enter_context(nc.Block())

        @block.sync
        def _(sp):
            def load(dst, src, s):
                sp.dma_start(dst, src).then_inc(s, 16)
            start = 2 * P
            load(self_first[:], t_in["self_first"], first_in)
            load(xT[:, 0:start], t_in["xT"][:, 0:start], first_in)
            load(self_rest[:], t_in["self_rest"], rest_in)
            load(xT[:, start:], t_in["xT"][:, start:], rest_in)
            load(cT[:], t_in["cT"], rest_in)
            load(others[:], t_in["others"], rest_in)
            load(bo_row[:], t_in["bo_row"], rest_in)
            load(xnat[:], t_in["xnat"], rest_in)
            sp.dma_start(w1[:], t_in["w1"].rearrange("e c f -> c e f")).then_inc(w_in, 16)
            sp.dma_start(w2[:], t_in["w2"].rearrange("e (j p) c -> p e j c", p=P)).then_inc(w_in, 16)
            with sp.Fori(0, PAIRS // 4) as m:
                for k in range(2):
                    sp.wait_ge(res_ready, 4 * m + 2 * k + 2)
                    sp.dma_start(out[bass.ds(4 * m + 2 * k, 2)].rearrange("o t c -> t o c"), res[k][:]).then_inc(out_done[k], 16)
            for k in range(2):
                sp.wait_ge(out_done[k], 16 * PAIRS // 4)

        @block.gpsimd
        def _(pool):
            for n in (A, B):
                nc.gpsimd.memset(QZ[n][:], 0.0)
                nc.gpsimd.memset(VB[n][:], 0.0)
            nc.gpsimd.memset(mhalf[:], -0.5)
            nc.gpsimd.memset(ones_row[:], 1.0).then_inc(zero_ready, 1)
            pool.wait_ge(zero_ready, 1)
            def stage(n, u):
                if isinstance(u, int) and u == 0 and n == A:
                    pool.wait_ge(first_in, 16 * FIRST)
                if isinstance(u, int) and u == 1 and n == A:
                    prepare_biases()
                need(pool, k_done[n], u)
                need(pool, v_done[n], u)
                if n == A:
                    need(pool, q_done[A], u)
                src = xt_view[n][:, bass.ds(u, 1)].rearrange("p o b k -> p (o b) k")
                nc.gpsimd.tensor_copy(xs[n][:], src.unsqueeze(2).broadcast_to([P, 2, 2, SEQ])).then_inc(xs_ready[n], 1)

            def power(n, u):
                need(pool, ve_ready[n], u + 1)
                nc.gpsimd.tensor_tensor(RS[n][:], VE[n][:], mhalf[:], ALU.pow).then_inc(rs_ready[n], 1)

            def floor(b, u):
                pool.wait_ge(zero_ready, 1)
                need(pool, e_ready[b], u + 1)
                half_p = PZ[A][:, b].rearrange("p h k -> p (h k)")
                nc.gpsimd.tensor_scalar(half_p, half_p, CLIP_FLOOR, None, ALU.max).then_inc(p_ready[A], 1)

            def keep_x1(u):
                need(pool, xn_ready[A], u + 1)
                if isinstance(u, int):
                    pool.wait_ge(bo_ready, 1)
                nc.gpsimd.tensor_tensor(x1b_all[:, bass.ds(u, 1)].rearrange("p o c -> p (o c)"), XN[A][:],
                                        bo_all[:], ALU.add).then_inc(x1b_ready, 1)

            def keep_x2(u):
                need(pool, xn_ready[B], u + 1)
                nc.gpsimd.tensor_copy(x2_all[:, bass.ds(u, 1)].rearrange("p o c -> p (o c)"), XN[B][:])\
                    .then_inc(x2_kept, 1)

            def prepare_biases():
                pool.wait_ge(rest_in, 16 * REST)
                nc.gpsimd.tensor_copy(bv_cols[:], bias[:, 2:3].broadcast_to([P, P])).then_inc(bv_ready, 1)
                nc.gpsimd.tensor_tensor(bk_masked[:], bias[:, 1:2].broadcast_to([P, 4]), hmask[:, :, 0], ALU.mult)\
                    .then_inc(bk_ready, 1)

            def iteration(at, read, once):
                at(0, stage, A)
                at(1, floor, 0)
                at(2, stage, B)
                at(1, floor, 1)
                at(2, power, A)
                at(2, keep_x1)
                at(4, power, B)
                at(4, keep_x2)

            pipeline(pool, iteration)

            for h in range(2):
                pool.wait_ge(gate_ready, h + 1)
                pool.wait_ge(disp_ready, 2 * h + 2)
                for b in range(2):
                    nc.gpsimd.tensor_tensor(half(gdisp, h)[:, :, b], half(disp, h)[:, :, b], by_slot(gate, h), ALU.mult)\
                        .then_inc(gdisp_ready, 1)

            with pool.Fori(0, PAIRS // 2) as m:
                for k in range(2):
                    pool.wait_ge(fve, 2 * m + k + 1)
                    nc.gpsimd.tensor_tensor(RS[k][:], VE[k][:], mhalf[:], ALU.pow).then_inc(frs, 1)

        @block.scalar
        def _(act):
            def spread_queries(n, u):
                need(act, q_done[n], u + 1)
                need(act, s_done[n], 2 * u)
                for g in range(4):
                    r = slice(32 * g, 32 * g + 32)
                    src = Q_bank[n][r].rearrange("p (b q) -> p b q", b=2)
                    if n == A:
                        last = nc.scalar.activation(QZ[n][r, :, g], src, ACT.Copy)
                    else:
                        last = nc.scalar.activation(QZ[n][r, :, g], src, ACT.Identity, bias=bias[r, 0:1])
                last.then_inc(qz_ready[n], 1)

            def spread_values(n, u):
                need(act, v_done[n], u + 1)
                need(act, num_done[n], u)
                src = V_bank[n].rearrange("p (m g h d) -> p m g h d", g=2, h=2, d=DH)
                dst = VB[n][:].rearrange("p m (h j) -> p m h j", h=2)
                for hl in range(2):
                    r = slice(64 * hl, 64 * hl + 64)
                    last = nc.scalar.activation(dst[r, :, :, DH * hl:DH * hl + DH], src[r, :, :, hl], ACT.Copy)
                last.then_inc(vb_ready[n], 1)

            def mask_keys(n, u):
                need(act, k_done[n], u + 1)
                need(act, s_done[n], 2 * u)
                if isinstance(u, int) and u == 0:
                    act.wait_ge(bk_ready, 1)
                for h in range(4):
                    last = nc.scalar.activation(KM[n][:, :, h], K_bank[n].rearrange("p (b k) -> p b k", b=2), ACT.Identity,
                                                bias=bk_masked[:, h:h + 1], scale=hmask[:, h, 0:1])
                last.then_inc(km_ready[n], 1)

            def exponentials(n, b, u):
                need(act, z_ready[n], 2 * u + b + 1)
                nc.scalar.activation(PZ[n][:, b], PZ[n][:, b], ACT.Exp, scale=SCALE)\
                    .then_inc(e_ready[b] if n == A else p_ready[B], 1)

            def turned_probs(n, b, u):
                need(act, t_done[n], 2 * u + b + 1)
                need(act, den_done[n], u)
                nc.scalar.activation(PT[n][:, b].rearrange("p m q -> p (m q)"), PT_bank[n][:], ACT.Copy)\
                    .then_inc(pt_ready[n], 1)

            def turned_x(n, u):
                need(act, xt_done[n], u + 1)
                if n == A:
                    need(act, q_done[B], u)
                    nc.scalar.activation(x1T[:].rearrange("p b q -> p (b q)"), XT_bank[n], ACT.Copy)\
                        .then_inc(xt_ready[n], 1)
                else:
                    need(act, lg_done, u)
                    nc.scalar.activation(x2T[:], XT_bank[n], ACT.Copy).then_inc(xt_ready[n], 1)

            def keep_logits(u):
                need(act, lg_done, u + 1)
                nc.scalar.activation(logits[:, bass.ds(u, 1)].rearrange("p o e -> p (o e)"), logit_bank,
                                     ACT.Copy).then_inc(lg_ready, 1)

            def keep_dispatched():
                with act.Fori(0, HALF // 2) as m:
                    for k in range(2):
                        act.wait_ge(d_done, 2 * m + k + 1)
                        nc.scalar.activation(slots_of(2 * m + k), dispatched(bank[2 * k]), ACT.Copy).then_inc(buf_ready, 1)

            def router_exponentials(h):
                act.wait_ge(rz_ready, h + 1)
                nc.scalar.activation(half(prob, h), half(rz, h), ACT.Exp).then_inc(rexp_ready, 1)

            act.wait_ge(zero_ready, 1)

            def iteration(at, read, once):
                once(PAIRS, router_exponentials, 0)
                at(0, spread_queries, A)
                at(3, exponentials, B, 0)
                at(1, turned_probs, A, 0)
                at(2, mask_keys, B)
                at(1, turned_probs, A, 1)
                at(3, turned_probs, B, 0)
                at(2, turned_x, A)
                at(3, exponentials, B, 1)
                at(0, spread_values, A)
                at(0, exponentials, A, 0)
                at(2, spread_queries, B)
                at(3, turned_probs, B, 1)
                once(PAIRS + 3, keep_dispatched)
                at(4, turned_x, B)
                at(4, keep_logits)
                at(2, spread_values, B)
                at(0, exponentials, A, 1)

            pipeline(act, iteration)

            router_exponentials(1)

            def hidden(h, j, m, k):
                e = 2 * m + k
                act.wait_ge(h_done, FJ * (E * h + e) + j + 1)
                need(act, ye_done[k], E // 2 * h + m)
                nc.scalar.activation(HT[k][:, j], bank[j][:, 0:HSLOT], ACT.Relu,
                                     bias=b1[:, bass.ds(e, 1), j]).then_inc(h_ready_act, 1)

            def keep_result(h, m, k):
                act.wait_ge(ye_done[k], E // 2 * h + m + 1)
                nc.scalar.activation(expert_result(h, 2 * m + k), bank[4 + k][:, 0:HSLOT].rearrange("p (n s) -> p n s", s=CAP),
                                     ACT.Identity, bias=b2[:, bass.ds(2 * m + k, 1)]).then_inc(y_ready, 1)

            def keep_turned(m, k, source):
                act.wait_ge(ygt_done, 2 * m + k + 1)
                need(act, c_done, 2 * m + k - 1)
                nc.scalar.activation(yg[k][0:BSLOT].rearrange("p n c -> p (n c)"), source[0:BSLOT, :], ACT.Copy)\
                    .then_inc(yg_ready, 1)

            def experts_first(m):
                for k in range(2):
                    for j in range(FJ):
                        hidden(0, j, m, k)
                    if k == 1:
                        keep_result(0, m, 0)
                    elif not isinstance(m, int) or m > 0:
                        keep_result(0, m - 1, 1)
            peeled(act, E // 2, experts_first)
            keep_result(0, E // 2 - 1, 1)

            def experts_second(m):
                for k in range(2):
                    keep_turned(m, k, bank[6])
                    for j in (0, 2):
                        hidden(1, j, m, k)
                    if k == 1:
                        keep_result(1, m, 0)
                    elif not isinstance(m, int) or m > 0:
                        keep_result(1, m - 1, 1)
            peeled(act, E // 2, experts_second)
            keep_result(1, E // 2 - 1, 1)
            with act.Fori(HALF // 2, PAIRS // 2) as m:
                for k in range(2):
                    keep_turned(m, k, bank[6 * (1 - k)])

        @block.tensor
        def _(pe):
            mm = nc.tensor.matmul

            def project_queries(n, u):
                need(pe, xs_ready[A] if n == A else xt_ready[A], u + 1)
                mm(Q_bank[n], wq[n], xs[A][:, :, 0] if n == A else x1T[:], start=True, stop=True).then_inc(q_done[n], 1)

            def project_keys(n, u):
                need(pe, xs_ready[n], u + 1)
                mm(K_bank[n], wk[n], xs[n][:, :, 0], start=True, stop=True).then_inc(k_done[n], 1)

            def project_values(n, u):
                need(pe, xs_ready[n], u + 1)
                for b in range(2):
                    last = mm(V_bank[n][:, P * b:P * b + P], xs[n][:, b], wv[n], start=True, stop=True)
                last.then_inc(v_done[n], 1)

            def scores(n, b, u):
                need(pe, qz_ready[n], u + 1)
                need(pe, km_ready[n], u + 1)
                need(pe, z_ready[n], 2 * u + b)
                if isinstance(u, int) and u == 0 and n == B and b == 0:
                    pe.wait_ge(bo_ready, 1)
                for gp in range(2):
                    last = mm(S_bank[n][:, 256 * gp:256 * gp + 256], QZ[n][:, b, 2 * gp:2 * gp + 2], KM[n][:, b],
                              start=True, stop=True)
                last.then_inc(s_done[n], 1)

            def turn_probs(n, b, u):
                if isinstance(u, int) and u == 0 and n == A and b == 0:
                    bias_out()
                need(pe, p_ready[n], 2 * u + b + 1)
                need(pe, pt_ready[n], 2 * u + b)
                for m in range(4):
                    last = nc.tensor.transpose(PT_bank[n][:, P * m:P * m + P], PZ[n][:, b, 2 * m:2 * m + 2].rearrange("p h k -> p (h k)"), ident)
                last.then_inc(t_done[n], 1)

            def weigh_values(n, b, u):
                need(pe, pt_ready[n], 2 * u + b + 1)
                need(pe, vb_ready[n], u + 1)
                for hp in range(2):
                    for g in range(4):
                        q = SEQ * (g % 2)
                        last = mm(num_bank[n][32 * g:32 * g + 32, SEQ * b:SEQ * b + SEQ], VB[n][:, 4 * b + g, 32 * hp:32 * hp + 32],
                                  PT[n][:, b, 2 * (g // 2) + hp, q:q + SEQ], start=(hp == 0), stop=(hp == 1))
                if b == 1:
                    last.then_inc(num_done[n], 1)

            def sum_weights(n, u):
                for hp in range(2):
                    for g in range(4):
                        q = SEQ * (g % 2)
                        last = mm(den_bank[n][32 * g:32 * g + 32], ones_sel[:, hp], PT[n][:, :, 2 * (g // 2) + hp, q:q + SEQ],
                                  start=(hp == 0), stop=(hp == 1))
                last.then_inc(den_done[n], 1)

            def project_out(n, u):
                need(pe, on_ready[n], u + 1)
                mm(Y_bank[n], ON[n][:], wo[n], start=True, stop=True).then_inc(y_done[n], 1)

            def turn_x(n, u):
                need(pe, xn_ready[n], u + 1)
                nc.tensor.transpose(XT_bank[n], XN[n][:], ident).then_inc(xt_done[n], 1)

            def route(u):
                need(pe, xt_ready[B], u + 1)
                mm(logit_bank, x2T[:], wr, start=True, stop=True).then_inc(lg_done, 1)

            def dispatch(p):
                h = p // HALF
                pe.wait_ge(disp_ready, 2 * h + 2)
                if h == 0:
                    pe.wait_ge(z_ready[A], 2 * PAIRS)
                    pe.wait_ge(pt_ready[A], 2 * PAIRS)
                pe.wait_ge(x2_kept, p + 1)
                need(pe, buf_ready, p - 1)
                to = bank[2 * (p % 2) if h == 0 else 6 + p % 2]
                mm(to[:, 0:DSLOT], x2_all[:, p], disp[:, p].rearrange("p b e s -> p (b e s)"),
                   start=True, stop=True).then_inc(d_done, 1)

            def hidden_read(h, e, j):
                if h == 0:
                    need(pe, h_ready_act, FJ * e + j + 1)
                elif j % 2 == 0:
                    need(pe, h_ready_act, FJ * E + 2 * e + j // 2 + 1)
                else:
                    need(pe, h_ready_dve, 2 * e + j // 2 + 1)

            def up(h, e):
                if h == 0 and e == 0:
                    pe.wait_ge(buf_ready, HALF)
                    pe.wait_ge(w_in, 32)
                    pe.wait_ge(z_ready[B], 2 * PAIRS)
                    pe.wait_ge(pt_ready[B], 2 * PAIRS)
                for j in range(FJ):
                    if e > 0:
                        hidden_read(h, e - 1, j)
                    elif h == 1:
                        hidden_read(0, E - 1, j)
                    mm(bank[j][:, 0:HSLOT], w1[:, e, P * j:P * j + P], buf[:, e, HSLOT * h:HSLOT * h + HSLOT],
                       start=True, stop=True).then_inc(h_done, 1)

            def dispatch_some(first, after):
                for p in range(first, after):
                    dispatch(p)

            def queue_places(h):
                pe.wait_ge(chosen_ready, h + 1)
                pe.wait_ge(z_ready[A], 2 * PAIRS)
                mm(bank[0 if h == 0 else 6][:, 0:HALF * E], before, half(chosen, h).rearrange("p u e -> p (u e)"),
                   start=True, stop=True).then_inc(pos_done, 1)

            pe.wait_ge(first_in, 16 * FIRST)

            def bias_out():
                pe.wait_ge(rest_in, 16 * REST)
                pe.wait_ge(bv_ready, 1)
                pe.wait_ge(zero_ready, 1)
                mm(S_bank[B][:, 0:D], bv_cols[:], wo[B], start=True, stop=False)
                mm(S_bank[B][:, 0:D], ones_row[:], bo_row[:], start=False, stop=True).then_inc(bo_sum, 1)

            def iteration(at, read, once):
                read((5, r_ready[B]), (5, on_ready[B]))
                at(4, sum_weights, B)
                read((5, lg_ready), (5, xt_ready[B]), (2, on_ready[A]), (1, km_ready[A]))
                at(0, project_keys, A)
                read((3, vb_ready[B]), (1, vb_ready[A]), (1, qz_ready[A]))
                at(0, project_queries, A)
                at(1, turn_probs, A, 0)
                read((2, r_ready[A]), (3, qz_ready[B]), (3, xt_ready[A]), (3, km_ready[B]))
                at(2, project_keys, B)
                at(3, scores, B, 1)
                at(0, scores, A, 0)
                once(PAIRS + 3, dispatch_some, 0, HALF // 2)
                read((4, on_ready[B]), (5, r_ready[B]))
                at(4, project_out, B)
                at(1, turn_probs, A, 1)
                read((0, qz_ready[A]), (3, vb_ready[B]), (1, vb_ready[A]))
                at(0, project_values, A)
                at(3, turn_probs, B, 0)
                read((0, km_ready[A]), (5, lg_ready), (5, xt_ready[B]), (2, on_ready[A]))
                at(1, weigh_values, A, 0)
                read((2, km_ready[B]), (2, r_ready[A]), (3, qz_ready[B]), (3, xt_ready[A]))
                at(2, turn_x, A)
                read((0, km_ready[A]), (5, lg_ready), (5, xt_ready[B]), (2, on_ready[A]))
                at(1, weigh_values, A, 1)
                read((0, km_ready[A]), (5, lg_ready), (5, xt_ready[B]), (2, on_ready[A]))
                at(1, sum_weights, A)
                read((2, xt_ready[A]), (2, km_ready[B]), (2, r_ready[A]), (3, qz_ready[B]))
                at(2, project_queries, B)
                read((4, r_ready[B]), (4, on_ready[B]))
                at(3, weigh_values, B, 0)
                at(0, scores, A, 1)
                read((0, vb_ready[A]), (0, qz_ready[A]), (3, vb_ready[B]))
                at(2, project_values, B)
                at(3, turn_probs, B, 1)
                at(2, scores, B, 0)
                once(PAIRS + 3, dispatch_some, HALF // 2, HALF)
                read((1, on_ready[A]), (0, km_ready[A]), (5, lg_ready), (5, xt_ready[B]))
                at(4, turn_x, B)
                read((2, qz_ready[B]), (2, xt_ready[A]), (2, km_ready[B]), (2, r_ready[A]))
                at(1, project_out, A)
                read((4, r_ready[B]), (4, on_ready[B]))
                at(3, weigh_values, B, 1)
                read((4, xt_ready[B]), (1, on_ready[A]), (0, km_ready[A]), (5, lg_ready))
                at(4, route)
                once(PAIRS + 1, queue_places, 0)

            pipeline(pe, iteration)

            def down(h, e):
                need(pe, y_ready, E * h + e - 1)
                for j in range(FJ):
                    hidden_read(h, e, j)
                    last = mm(bank[4 + e % 2][:, 0:HSLOT], w2[:, e, j], HT[e % 2][:, j], start=(j == 0), stop=(j == FJ - 1))
                last.then_inc(ye_done[e % 2], 1)

            def turn_pair(p):
                h = p // HALF
                pe.wait_ge(y_ready, E * (h + 1))
                pe.wait_ge(gdisp_ready, 2 * (h + 1))
                need(pe, yg_ready, p if p <= HALF else p - 1)
                to = bank[6 if p < HALF or p % 2 == 0 else 0]
                for b in range(2):
                    nc.tensor.transpose(to[0:BSLOT, P * b:P * b + P], yexp[:, 2 * p + b].rearrange("p e s -> p (e s)"), ident)
                    last = nc.tensor.transpose(to[0:BSLOT, P * (2 + b):P * (3 + b)],
                                               gdisp[:, p, b].rearrange("p e s -> p (e s)"), ident)
                last.then_inc(ygt_done, 1)

            def combine(p):
                k = p % 2
                pe.wait_ge(yg_ready, p + 1)
                need(pe, fr_ready, p if p <= HALF else p - 1)
                to = bank[7 if p < HALF or k == 0 else 1]
                for b in range(2):
                    last = mm(to[:, 0:D], yg[k][0:BSLOT, 2 + b], yg[k][0:BSLOT, b], start=(b == 0), stop=(b == 1))
                last.then_inc(c_done, 1)

            up(0, 0)
            for e in range(1, E):
                up(0, e)
                if e == E // 2:
                    queue_places(1)
                down(0, e - 1)
                if e >= E - 2:
                    for p in range(HALF + HALF // 2 * (e - E + 2), HALF + HALF // 2 * (e - E + 3)):
                        dispatch(p)
            down(0, E - 1)
            pe.wait_ge(buf_ready, PAIRS)
            up(1, 0)
            turn_pair(0)
            combine(0)
            for e in range(1, E):
                turn_pair(e)
                up(1, e)
                combine(e)
                down(1, e - 1)
            down(1, E - 1)
            turn_pair(HALF)
            for p in range(HALF + 1, PAIRS):
                turn_pair(p)
                combine(p - 1)
            combine(PAIRS - 1)

        @block.vector
        def _(dve):
            V = nc.vector

            def mask_keys(n, u):
                need(dve, k_done[n], u + 1)
                need(dve, s_done[n], 2 * u)
                src = K_bank[n].rearrange("p (b k) -> p b k", b=2)
                if n == A:
                    last = V.tensor_tensor(KM[n][:], src.unsqueeze(2).broadcast_to([P, 2, 4, SEQ]), headed(hmask, 2), ALU.mult)
                else:
                    for b in range(2):
                        last = V.scalar_tensor_tensor(KM[n][:, b], headed(src[:, b], 4), bias[:, 1:2], hmask, ALU.add, ALU.mult)
                last.then_inc(km_ready[n], 1)

            def row_max(n, b, u):
                need(dve, s_done[n], 2 * u + b + 1)
                V.tensor_reduce(MX[n][:, b], S_bank[n][:].rearrange("p (h k) -> p h k", k=SEQ), AX.X, ALU.max)\
                    .then_inc(mx_ready[n], 1)

            def less_max(n, b, u):
                need(dve, mx_ready[n], 2 * u + b + 1)
                need(dve, t_done[n], 2 * u + b - 1)
                V.tensor_tensor(PZ[n][:, b], S_bank[n][:].rearrange("p (h k) -> p h k", k=SEQ),
                                MX[n][:, b].unsqueeze(2).broadcast_to([P, 8, SEQ]), ALU.subtract).then_inc(z_ready[n], 1)

            def add_eps(u):
                need(dve, den_done[A], u + 1)
                V.tensor_scalar(DEN[:], den_bank[A], SOFTMAX_EPS, None, ALU.add).then_inc(eps_added, 1)

            def invert(n, u):
                if n == A:
                    need(dve, eps_added, u + 1)
                else:
                    need(dve, den_done[B], u + 1)
                V.reciprocal(REC[n][:], DEN[:] if n == A else den_bank[B]).then_inc(rec_ready[n], 1)

            def normalise(n, u):
                need(dve, rec_ready[n], u + 1)
                need(dve, y_done[n], u)
                V.tensor_tensor(ON[n][:], num_bank[n], REC[n][:], ALU.mult).then_inc(on_ready[n], 1)

            def residual(n, u):
                if isinstance(u, int) and u == 0 and n == A:
                    dve.wait_ge(rest_in, 16 * REST)
                    dve.wait_ge(bo_sum, 1)
                    V.tensor_copy(bo_all[:], S_bank[B][:, 0:D]).then_inc(bo_ready, 1)
                need(dve, y_done[n], u + 1)
                if n == A:
                    x = xnat[:, bass.ds(u, 1)]
                else:
                    need(dve, x1b_ready, u + 1)
                    x = x1b_all[:, bass.ds(u, 1)]
                V.tensor_tensor(R[n][:], Y_bank[n], x.rearrange("p o c -> p (o c)"), ALU.add).then_inc(r_ready[n], 1)

            def statistics(n, u):
                need(dve, r_ready[n], u + 1)
                V.bn_stats(ST[n][:], R[n][:]).then_inc(st_ready[n], 1)

            def mean_variance(n, u):
                dve.wait_ge(rest_in, 16 * REST)
                need(dve, st_ready[n], u + 1)
                V.bn_aggr(MV[n][:], ST[n][:]).then_inc(mv_ready[n], 1)

            def variance_eps(n, u):
                need(dve, mv_ready[n], u + 1)
                V.tensor_scalar(VE[n][:], MV[n][:, 1:2], LN_EPS, None, ALU.add).then_inc(ve_ready[n], 1)

            def layer_norm(n, u):
                need(dve, rs_ready[n], u + 1)
                need(dve, xt_done[n], u)
                need(dve, x1b_ready if n == A else x2_kept, u)
                V.tensor_scalar(XN[n][:], R[n][:], MV[n][:, 0:1], RS[n][:], ALU.subtract, ALU.mult)\
                    .then_inc(xn_ready[n], 1)

            dve.wait_ge(first_in, 16 * FIRST)

            count = [0]

            def then(ins):
                count[0] += 1
                ins.then_inc(router, 1)
                dve.wait_ge(router, count[0])

            def wide(t, h):
                return half(t, h).unsqueeze(2).broadcast_to([P, HALF, E])

            def flat(t, h):
                return half(t, h).rearrange("p u e -> p (u e)")

            def router_logits(h):
                dve.wait_ge(lg_ready, HALF * (h + 1))
                then(V.tensor_reduce(half(rmax, h), half(logits, h), AX.X, ALU.max))
                V.tensor_tensor(half(rz, h), half(logits, h), wide(rmax, h), ALU.subtract).then_inc(rz_ready, 1)

            def router_probs(h):
                dve.wait_ge(rexp_ready, h + 1)
                then(V.tensor_reduce(half(rmax, h), half(prob, h), AX.X, ALU.add))
                then(V.reciprocal(half(rmax, h), half(rmax, h)))
                then(V.tensor_tensor(half(prob, h), half(prob, h), wide(rmax, h), ALU.mult))

            def choose(h, k):
                left = prob if k == 0 else rz
                then(V.tensor_reduce(half(rmax, h), half(left, h), AX.X, ALU.max))
                then(V.tensor_tensor(half(cand, h), half(left, h), wide(rmax, h), ALU.is_equal))
                then(V.tensor_tensor(half(cand, h), half(cand, h), headed(rank, HALF), ALU.mult))
                then(V.tensor_reduce(half(rmax, h), half(cand, h), AX.X, ALU.max))
                then(V.tensor_tensor(half(pick[k], h), half(cand, h), wide(rmax, h), ALU.is_equal))
                if k == 0:
                    then(V.scalar_tensor_tensor(flat(rz, h), flat(pick[0], h), -2.0, flat(prob, h), ALU.mult, ALU.add))

            def choices(h):
                V.tensor_tensor(half(chosen, h), half(pick[0], h), half(pick[1], h), ALU.add).then_inc(chosen_ready, 1)
                dve.wait_ge(chosen_ready, h + 1)
                V.tensor_tensor(half(gate, h), half(prob, h), half(chosen, h), ALU.mult).then_inc(gate_ready, 1)

            def places(h):
                dve.wait_ge(pos_done, h + 1)
                then(V.scalar_tensor_tensor(flat(place, h), bank[0 if h == 0 else 6][:, 0:HALF * E], 1.0, flat(chosen, h),
                                            ALU.add, ALU.mult))
                then(V.tensor_scalar(flat(place, h), flat(place, h), -1.0, None, ALU.add))

            def slots(h):
                for b in range(2):
                    number = slotno[:, CAP * b:CAP * b + CAP].unsqueeze(1).unsqueeze(1).broadcast_to([P, HALF, E, CAP])
                    V.tensor_tensor(half(disp, h)[:, :, b], number, by_slot(place, h), ALU.is_equal).then_inc(disp_ready, 1)

            def iteration(at, read, once):
                once(PAIRS, router_logits, 0)
                at(2, statistics, A)
                at(0, mask_keys, A)
                at(4, invert, B)
                at(2, mean_variance, A)
                once(PAIRS + 1, router_probs, 0)
                at(4, normalise, B)
                at(2, variance_eps, A)
                at(3, row_max, B, 1)
                at(4, residual, B)
                once(PAIRS + 1, choose, 0, 0)
                at(2, layer_norm, A)
                at(3, less_max, B, 1)
                at(4, statistics, B)
                at(0, row_max, A, 0)
                at(4, mean_variance, B)
                once(PAIRS + 1, choose, 0, 1)
                once(PAIRS + 2, places, 0)
                at(4, variance_eps, B)
                at(0, less_max, A, 0)
                at(1, add_eps)
                at(4, layer_norm, B)
                once(PAIRS + 1, choices, 0)
                once(PAIRS + 2, slots, 0)
                at(1, invert, A)
                at(0, row_max, A, 1)
                at(1, normalise, A)
                at(0, less_max, A, 1)
                at(2, row_max, B, 0)
                at(1, residual, A)
                at(2, less_max, B, 0)

            pipeline(dve, iteration)

            router_logits(1)
            router_probs(1)
            choose(1, 0)
            choose(1, 1)
            choices(1)
            places(1)
            slots(1)
            with dve.Fori(HALF // 2, PAIRS // 2) as m:
                for k in range(2):
                    dve.wait_ge(d_done, 2 * m + k + 1)
                    V.tensor_copy(slots_of(2 * m + k), dispatched(bank[6 + k])).then_inc(buf_ready, 1)

            def hidden(m, n):
                k = n % 2
                for j in (1, 3):
                    dve.wait_ge(h_done, FJ * (4 * m + n) + FJ * E + j + 1)
                    dve.wait_ge(ye_done[k], E // 2 + 2 * m + n // 2)
                    V.tensor_scalar(HT[k][:, j], bank[j][:, 0:HSLOT], b1[:, bass.ds(4 * m + n, 1), j], 0.0, ALU.add, ALU.max)\
                        .then_inc(h_ready_dve, 1)

            def add_up(m, n, source):
                p = 4 * m + n
                dve.wait_ge(c_done, p + 1)
                need(dve, res_ready, p - 2)
                need(dve, fst, p)
                V.tensor_tensor(total[n][:], source[:, 0:D], x2_all[:, bass.ds(p, 1)].rearrange("p o c -> p (o c)"),
                                ALU.add).then_inc(fr_ready, 1)

            def final_statistics(m, n):
                k, p = n % 2, 4 * m + n
                dve.wait_ge(fr_ready, p + 1)
                need(dve, fmv, p - 1)
                V.bn_stats(ST[k][:], total[n][:]).then_inc(fst, 1)

            def final_mean_variance(k, count):
                dve.wait_ge(rest_in, 16 * REST)
                dve.wait_ge(fst, count)
                V.bn_aggr(MV[k][:], ST[k][:]).then_inc(fmv, 1)

            def final_variance_eps(m, n):
                k, p = n % 2, 4 * m + n
                dve.wait_ge(fmv, p + 1)
                V.tensor_scalar(VE[k][:], MV[k][:, 1:2], LN_EPS, None, ALU.add).then_inc(fve, 1)

            def finish(m, n):
                k, p = n % 2, 4 * m + n
                dve.wait_ge(frs, p + 1)
                need(dve, out_done[n // 2], 16 * m)
                V.tensor_scalar(res[n // 2][:, k], total[n][:], MV[k][:, 0:1], RS[k][:], ALU.subtract, ALU.mult)\
                    .then_inc(res_ready, 1)

            def before_it(step, m, n, back):
                if n >= back:
                    step(m, n - back)
                elif not isinstance(m, int) or m > 0:
                    step(m - 1, n - back + 4)

            def close_pair(m, n, source):
                add_up(m, n, source)
                if not isinstance(m, int) or m > 0 or n > 0:
                    final_mean_variance(1 - n % 2, 4 * m + n)
                final_statistics(m, n)
                before_it(finish, m, n, 2)
                before_it(final_variance_eps, m, n, 1)

            def second_half(m):
                for n in range(4):
                    hidden(m, n)
                    close_pair(m, n, bank[7])
            peeled(dve, HALF // 4, second_half)
            with dve.Fori(HALF // 4, PAIRS // 4) as m:
                for n in range(4):
                    close_pair(m, n, bank[7 if n % 2 == 0 else 1])
            last = PAIRS // 4 - 1
            dve.wait_ge(res_ready, PAIRS - 2)
            final_mean_variance(1, PAIRS)
            final_variance_eps(last, 3)
            finish(last, 2)
            finish(last, 3)


FIRST, REST = 2, 6
OTHERS = (("wq", D), ("wk", D), ("wv", D), ("wo", D), ("before", P), ("wr", E), ("b1", E * FJ), ("b2", E), ("bias", 4),
          ("rank", E), ("slotno", PSLOT))


def kernel(x, ctx_1024, L0_attn_Wqkv, L0_attn_Wout, L0_xattn_Wq, L0_xattn_bq, L0_xattn_Wk, L0_xattn_bk, L0_xattn_Wv,
           L0_xattn_bv, L0_xattn_Wo, L0_xattn_bo, L0_ffn_Wr, L0_ffn_W1, L0_ffn_b1, L0_ffn_W2, L0_ffn_b2):
    import concourse.bacc as bacc
    from concourse.bass_utils import run_bass_kernel_spmd

    c = np.ascontiguousarray

    x, ctx_1024 = np.asarray(x), np.asarray(ctx_1024)
    wqkv = np.asarray(L0_attn_Wqkv).T
    row = np.arange(P)
    tok, batch = row % SEQ, row // SEQ
    hh = (row // DH) % 4
    f = np.float32
    slot = np.where(batch[:, None, None] == np.arange(2)[None, :, None], np.arange(CAP)[None, None, :], -2)
    heads = np.broadcast_to((hh[:, None, None] == np.arange(4)[None, :, None]), (P, 4, SEQ)).reshape(P, -1).astype(f)
    sums = np.broadcast_to((np.arange(4)[None, None, :, None] == 2 * np.arange(2)[None, :, None, None]
                            + batch[:, None, None, None]), (P, 2, 4, DH)).reshape(P, -1).astype(f)
    small = {
        "wq": np.asarray(L0_xattn_Wq).T, "wk": np.asarray(L0_xattn_Wk).T,
        "wv": np.asarray(L0_xattn_Wv).T, "wo": np.asarray(L0_xattn_Wo).T,
        "bias": np.stack([np.asarray(b) for b in (L0_xattn_bq, L0_xattn_bk, L0_xattn_bv, L0_xattn_bo)], axis=1),
        "wr": np.asarray(L0_ffn_Wr),
        "b1": np.asarray(L0_ffn_b1).reshape(E, FJ, P).transpose(2, 0, 1),
        "b2": np.asarray(L0_ffn_b2).T,
        "before": ((tok[:, None] < tok[None, :]) & (batch[:, None] == batch[None, :])).astype(f),
        "rank": np.broadcast_to(E - np.arange(E), (P, E)).astype(f),
        "slotno": slot.reshape(P, PSLOT).astype(f),
    }
    arrays = {
        "xT": c(x.reshape(PAIRS * P, D).T),
        "cT": c(ctx_1024.reshape(PAIRS * P, D).T),
        "xnat": c(x.reshape(PAIRS, P, D).transpose(1, 0, 2)),
        "self_first": c(np.concatenate([wqkv[:, 0:3 * D], heads], axis=1)),
        "self_rest": c(np.concatenate([np.eye(P, dtype=f), np.asarray(L0_attn_Wout).T, sums], axis=1)),
        "others": c(np.concatenate([small[name].reshape(P, n) for name, n in OTHERS], axis=1)),
        "bo_row": c(np.asarray(L0_xattn_bo)[None, :]),
        "w1": c(np.asarray(L0_ffn_W1)), "w2": c(np.asarray(L0_ffn_W2)),
    }
    nc = bacc.Bacc("TRN2", target_bir_lowering=False, num_devices=1)
    t_in = {k: nc.dram_tensor(f"in_{k}", v.shape, F32, kind="ExternalInput").ap() for k, v in arrays.items()}
    out = nc.dram_tensor("out", (PAIRS, P, D), F32, kind="ExternalOutput").ap()
    decoder_kernel(nc, t_in, out)
    r = run_bass_kernel_spmd(nc, [{f"in_{k}": v for k, v in arrays.items()}], core_ids=[0])
    return r.results[0]["out"].reshape(BATCH, SEQ, D)
```
